# Optimizing a Trainium2 kernel written in Bass

```python
import numpy as np
import jax
import jax.numpy as jnp

def _softmax(x, axis=-1):
    return jax.nn.softmax(x, axis=axis)

def _gelu(x):
    return jax.nn.gelu(x, approximate=True)

def _silu(x):
    return jax.nn.silu(x)

def _sigmoid(x):
    return jax.nn.sigmoid(x)

def _layernorm(x, axis=-1, eps=1e-05):
    m = jnp.mean(x, axis=axis, keepdims=True)
    v = jnp.var(x, axis=axis, keepdims=True)
    return (x - m) / jnp.sqrt(v + eps)

def _scatter_add(tgt, idx, src, axis=0):
    return tgt.at[idx].add(src)

def _segment_sum(src, seg, n):
    return jax.ops.segment_sum(src, seg, n)
kernel_name = 'mk_recurrent_d1_jaxref_r8_a9fac0'

def setup_inputs(seed: int=0):
    np.random.seed(seed)
    _w = jnp.asarray

    def _L0_attn_setup():
        import jax, jax.numpy as jnp
        import numpy as np
        HEADS = 32
        key = jax.random.key(seed)
        ks = jax.random.split(key, 5)
        H = 512
        B, S = (2, 256)
        w_scale = 1.0 / np.sqrt(H)
        return {'x': jax.random.normal(ks[0], (B, S, H), dtype=jnp.float32), 'attn_qkvw': jax.random.normal(ks[1], (H, 3 * H), dtype=jnp.float32) * w_scale, 'attn_qkvb': jax.random.normal(ks[2], (3 * H,), dtype=jnp.float32) * 0.02, 'attn_ow': jax.random.normal(ks[3], (H, H), dtype=jnp.float32) * w_scale, 'attn_ob': jax.random.normal(ks[4], (H,), dtype=jnp.float32) * 0.02}
    _L0_attn_in = _L0_attn_setup()

    def _L0_ffn_setup():
        import jax, jax.numpy as jnp
        import numpy as np
        IN_F = 512
        OUT_F = 512
        N_CLUSTERS = 64
        THRESHOLD = 0.01
        TEMPERATURE = 0.1
        BATCH, SEQ = (4, 256)
        key = jax.random.key(seed)
        k1, k2, k3, k4, k5 = jax.random.split(key, 5)
        s = 1.0 / np.sqrt(IN_F)
        return {'input': jax.random.normal(k1, (BATCH, SEQ, IN_F), dtype=jnp.float32), 'weight': jax.random.normal(k2, (OUT_F, IN_F), dtype=jnp.float32) * s, 'bias': jax.random.uniform(k3, (OUT_F,), dtype=jnp.float32, minval=-s, maxval=s), 'centroids': jax.random.normal(k4, (N_CLUSTERS, IN_F), dtype=jnp.float32) * s, 'assignments': jax.random.randint(k5, (OUT_F,), 0, N_CLUSTERS, dtype=jnp.int32)}
    _L0_ffn_in = _L0_ffn_setup()
    _d = {'L0_attn_x': _L0_attn_in['x'], 'L0_attn_attn_qkvw': _L0_attn_in['attn_qkvw'], 'L0_attn_attn_qkvb': _L0_attn_in['attn_qkvb'], 'L0_attn_attn_ow': _L0_attn_in['attn_ow'], 'L0_attn_attn_ob': _L0_attn_in['attn_ob'], 'L0_ffn_weight': _L0_ffn_in['weight'], 'L0_ffn_bias': _L0_ffn_in['bias'], 'L0_ffn_centroids': _L0_ffn_in['centroids'], 'L0_ffn_assignments': _L0_ffn_in['assignments']}
    _x0 = _d['L0_attn_x']
    _d['L0_attn_x'] = jax.random.normal(jax.random.fold_in(jax.random.key(seed), 1), (2, 512, 512), dtype=_x0.dtype)
    del _x0
    return _d

def reference(L0_attn_x, L0_attn_attn_qkvw, L0_attn_attn_qkvb, L0_attn_attn_ow, L0_attn_attn_ob, L0_ffn_weight, L0_ffn_bias, L0_ffn_centroids, L0_ffn_assignments):

    def _L0_attn_ref(x, attn_qkvw, attn_qkvb, attn_ow, attn_ob):
        import jax, jax.numpy as jnp
        import numpy as np
        HEADS = 32
        B, S, H = x.shape
        hd = H // HEADS
        scale = 1.0 / np.sqrt(hd)
        qkv = x @ attn_qkvw + attn_qkvb
        qkv = qkv.reshape(B, S, 3, HEADS, hd)
        q = jnp.transpose(qkv[:, :, 0], (0, 2, 1, 3))
        k = jnp.transpose(qkv[:, :, 1], (0, 2, 1, 3))
        v = jnp.transpose(qkv[:, :, 2], (0, 2, 1, 3))
        scores = jnp.einsum('bhqd,bhkd->bhqk', q, k) * scale
        probs = jax.nn.softmax(scores, axis=-1)
        ctx = jnp.einsum('bhqk,bhkd->bhqd', probs, v)
        ctx = jnp.transpose(ctx, (0, 2, 1, 3)).reshape(B, S, H)
        return ctx @ attn_ow + attn_ob

    def _L0_ffn_ref(input, weight, bias, centroids, assignments):
        import jax, jax.numpy as jnp
        import numpy as np
        IN_F = 512
        OUT_F = 512
        N_CLUSTERS = 64
        THRESHOLD = 0.01
        TEMPERATURE = 0.1
        BATCH, SEQ = (4, 256)
        shape = input.shape
        x = input.reshape(-1, shape[-1])
        dots = jax.nn.softmax(x @ centroids.T / TEMPERATURE, axis=-1)
        hits = dots > THRESHOLD
        query_sel = jnp.any(hits, axis=1)
        cluster_sel = jnp.any(hits, axis=0)
        row_sel = cluster_sel[assignments]
        dense = x @ weight.T + bias
        out = jnp.where(query_sel[:, None] & row_sel[None, :], dense, jnp.zeros((), dense.dtype))
        return out.reshape(*shape[:-1], -1)
    x = L0_attn_x
    xn = _layernorm(x, axis=-1)
    s = _L0_attn_ref(xn, L0_attn_attn_qkvw, L0_attn_attn_qkvb, L0_attn_attn_ow, L0_attn_attn_ob)
    g = _silu(_L0_ffn_ref(xn, L0_ffn_weight, L0_ffn_bias, L0_ffn_centroids, L0_ffn_assignments))
    x = x + s * g
    return x

_drawn_inputs = setup_inputs


def setup_inputs(seed=0):
    import zlib

    import numpy as np

    out = dict(_drawn_inputs(seed))
    spreads = {}
    factors = {'L0_attn_attn_qkvb': 3.076, 'L0_attn_attn_ob': 3.149, 'L0_ffn_bias': 30.817}
    for name, (base, spread) in spreads.items():
        noise = np.random.default_rng([zlib.crc32(name.encode()), seed]).standard_normal(out[name].shape)
        drawn = base * np.exp(spread * noise) if base else spread * noise
        out[name] = jnp.asarray(drawn.astype(out[name].dtype))
    for name, factor in factors.items():
        out[name] = (out[name] * factor).astype(out[name].dtype)
    return out
```

```python
from contextlib import ExitStack

import concourse.bass as bass
from concourse import mybir

F32 = mybir.dt.float32
F32R = mybir.dt.float32r
BF16 = mybir.dt.bfloat16
I32 = mybir.dt.int32
ALU = mybir.AluOpType
ACT = mybir.ActivationFunctionType
AX = mybir.AxisListType

P = 128
BANK = 512
BANKS = 8


def build(nc, x, qkvw, qkvb, ow, ob, fw, fb, cent, assign, out):
    B, S, H = x.shape
    N = fw.shape[0]
    CL = cent.shape[0]
    HD = 16
    HEADS = H // HD
    T = B * S // P
    TB = S // P
    KC = H // P
    OCT = P // HD
    GROUPS = B * HEADS // OCT
    OPB = GROUPS // B
    HALF = OCT // 2
    EPS = 1e-5
    SHARP = 10.0
    HIT = 0.01
    SCALE = HD ** -0.5
    ROWS_MAX, ROW_SHIFT, ROWS_EXP = 96, 96, 98
    LOAD = 8 * 16
    assert S == BANK and N == BANK and H == 4 * P and T == 8 and KC == TB == 4 and CL == 64

    x_t = x.rearrange("b (t p) h -> p (b t) h", p=P)
    out_t = out.rearrange("b (t p) h -> p (b t) h", p=P)
    w_c = qkvw.rearrange("(c p) n -> p c n", p=P)

    JOB_XT, JOB_WT, JOB_CENT, JOB_LOGITS = 0, 8, 12, 13
    JOB_DENSE = [14, 15, 16, 18, 20, 21, 22, 23]
    JOB_COUNT, JOB_ROWSEL, JOB_QK, JOB_V = 17, 19, 24, 40
    JOBS = 48
    SPLITS_A = 13
    qk_jobs = [(g, which) for g in range(GROUPS) for which in range(2)]

    with ExitStack() as ctx:
        def sem(name):
            return ctx.enter_context(nc.semaphore(name))

        def sems(name, n):
            return [sem(f"{name}{i}") for i in range(n)]

        start = (nc.sbuf_base + 63) // 64 * 64
        KB = 1024

        def at(name, offset, shape, dt):
            return nc.alloc_sbuf_tensor_at(name, shape, dt, offset=start + offset)

        QK, V, G, X, STAGE, WHI, WLO, XT, SMALL = 0, 64 * KB, 80 * KB, 96 * KB, 112 * KB, 124 * KB, 148 * KB, 172 * KB, 204 * KB
        q_hi = at("q_hi", QK, [P, GROUPS, S], F32R)
        q_lo = at("q_lo", QK + 16 * KB, [P, GROUPS, S], F32R)
        k_hi = at("k_hi", QK + 32 * KB, [P, GROUPS, S], F32R)
        k_lo = at("k_lo", QK + 48 * KB, [P, GROUPS, S], F32R)
        v_all = at("v_all", V, [P, GROUPS, TB, P], F32)
        gate = at("gate", G, [P, T, N], F32)
        xn = at("xn", X, [P, T, H], F32)
        gate_exp = at("gate_exp", X, [P, T, N], F32)
        w_stage = at("w_stage", STAGE, [P, 2, 3 * H], F32)
        w_hi = at("w_hi", WHI, [P, KC, 3 * H], F32R)
        w_lo = at("w_lo", WLO, [P, KC, 3 * H], F32R)
        xt_hi = at("xt_hi", XT, [P, KC, T * P], F32R)
        xt_lo = at("xt_lo", XT + 16 * KB, [P, KC, T * P], F32R)
        fw_raw = at("fw_raw", QK, [P, KC, H], F32)
        fwt_hi = at("fwt_hi", QK + 8 * KB, [P, KC, N], F32R)
        fwt_lo = at("fwt_lo", QK + 16 * KB, [P, KC, N], F32R)
        cent_raw = at("cent_raw", QK + 24 * KB, [CL, H], F32)
        centt_hi = at("centt_hi", QK + 26 * KB, [P, KC, CL], F32R)
        centt_lo = at("centt_lo", QK + 27 * KB, [P, KC, CL], F32R)
        qkb_raw = at("qkb_raw", QK + 28 * KB, [2 * KC, P], F32)
        logit = at("logit", V, [P, T, CL], F32)
        expo = at("expo", V + 2 * KB, [P, T, CL], F32)
        hits = at("hits", V + 4 * KB, [P, T, CL], BF16)
        onehot = at("onehot", V + 5 * KB, [CL, N], BF16)
        assign_b = at("assign_b", V + 6 * KB, [CL, N], I32)
        row_sel = at("row_sel", V + 8 * KB, [P, N], F32)
        fb_b = at("fb_b", V + 10 * KB, [P, N], F32)
        ident = at("ident", SMALL, [P, P], F32)
        row_bias = at("row_bias", SMALL + 512, [P, N], F32)
        small = SMALL + 512 + 2 * KB
        ones_bf = at("ones_bf", small, [P, P], BF16)
        cl_sel = at("cl_sel", small + 256, [CL, P], BF16)
        stats = at("stats", small + 512, [P, T, 6], F32)
        mv = at("mv", small + 704, [P, T, 2], F32)
        var_eps = at("var_eps", small + 768, [P, T], F32)
        rstd = at("rstd", small + 800, [P, T], F32)
        neg_half = at("neg_half", small + 832, [P, T], F32)
        qkb = at("qkb", small + 864, [P, 2 * KC], F32)
        lmax = at("lmax", small + 896, [P, T], F32)
        thr = at("thr", small + 928, [P, T], F32)
        q_sel = at("q_sel", small + 960, [P, T], F32)
        zeros = at("zeros", small + 1056, [P, TB], F32)
        iota_i = at("iota_i", small + 992, [CL, 1], I32)
        iota_f = at("iota_f", small + 1024, [CL, 1], F32)
        q_stack = at("q_stack", X, [P, OCT, S], F32R)
        k_stack = at("k_stack", STAGE, [P, OCT, S], F32R)
        b0 = STAGE + 16 * KB
        probs = at("probs", b0, [P, HALF, HALF, S], F32)
        v_ring = at("v_ring", b0 + 32 * KB, [P, 2, TB, HALF, 2 * HD], F32)
        ctx_raw = at("ctx_raw", b0 + 36 * KB, [P, 2, S], F32)
        ctx_c = at("ctx_c", b0 + 40 * KB, [P, S], F32)
        den_c = at("den_c", b0 + 42 * KB, [P, S], F32)
        ctx_n = at("ctx_n", b0 + 44 * KB, [P, S], F32)
        shift_row = at("shift_row", b0 + 46 * KB, [2 * TB, HALF, P], F32)
        ow_raw = at("ow_raw", b0 + 48 * KB, [P, KC, H], F32)
        x_res = at("x_res", b0 + 56 * KB, [P, T, H], F32)
        ob_gate = at("ob_gate", b0 + 72 * KB, [P, H], F32)
        neg_max = at("neg_max", b0 + 74 * KB, [P, OCT, TB], F32)
        shift = at("shift", b0 + 74 * KB + 128, [P, OCT, 2 * TB], F32)
        ow_hi = at("ow_hi", V, [P, KC, H], F32R)
        ow_lo = at("ow_lo", V + 8 * KB, [P, KC, H], F32R)
        ctx_hi, ctx_lo = q_hi, q_lo

        pairs = [ctx.enter_context(nc.psum_tensor(f"banks{2 * i}", [P, 2, BANK], F32)) for i in range(4)]
        bank = [pairs[i // 2][:, i % 2, :] for i in range(BANKS)]
        max_tile = [pairs[0], pairs[1]]
        exp_tile = [bank[4], bank[5]]
        ctx_bank, turn_bank = bank[6], bank[7]
        out_bank = [bank[i] for i in (0, 1, 2, 3, 4, 5, 7, 6)]

        x_loaded = sems("x_loaded", T)
        fw_loaded, cent_loaded, small_loaded = sem("fw_loaded"), sem("cent_loaded"), sem("small_loaded")
        w_loaded = sems("w_loaded", KC)
        consts_ready, iota_ready = sem("consts_ready"), sem("iota_ready")
        stats_done, aggr_done, var_ready, rstd_ready, xn_ready = (
            sem("stats_done"), sem("aggr_done"), sem("var_ready"), sem("rstd_ready"), sem("xn_ready"))
        onehot_ready = sem("onehot_ready")
        job_ready, hi_ready, job_evacuated = sem("job_ready"), sem("hi_ready"), sem("job_evacuated")
        dve_step, pool_step = sem("dve_step"), sem("pool_step")
        exp_ready, hits_ready = sem("exp_ready"), sem("hits_ready")
        w_hi_ready, w_lo_ready = sem("w_hi_ready"), sem("w_lo_ready")
        masked_ready, gate_exp_ready, gate_ready = sem("masked_ready"), sem("gate_exp_ready"), sem("gate_ready")
        pads_ready = sem("pads_ready")
        stack_loaded = sems("stack_loaded", OCT)
        shift_loaded = sems("shift_loaded", OCT)
        max_scores_ready, maxes_ready, shift_split = sem("max_scores_ready"), sem("maxes_ready"), sem("shift_split")
        shift_turned, shift_copied = sem("shift_turned"), sem("shift_copied")
        scores_ready, probs_ready, probs_used = sem("scores_ready"), sem("probs_ready"), sem("probs_used")
        v_ready, ctx_evacuated = sem("v_ready"), sem("ctx_evacuated")
        compact_loaded = sems("compact_loaded", 2)
        gate_den_ready, gate_inverted, den_inverted = sem("gate_den_ready"), sem("gate_inverted"), sem("den_inverted")
        ctx_divided, ctx_hi_ready, ctx_split = sem("ctx_divided"), sem("ctx_hi_ready"), sem("ctx_split")
        shift_hi_ready = sem("shift_hi_ready")
        late_loaded = sem("late_loaded")
        ow_ready, rest_ready, rest_step = sem("ow_ready"), sem("rest_ready"), sem("rest_step")
        out_tile_ready, gated_ready, out_ready, out_stored = (
            sem("out_tile_ready"), sem("gated_ready"), sem("out_ready"), sem("out_stored"))

        block = ctx.enter_context(nc.Block())

        @block.sync
        def _(sp):
            for t in range(T):
                sp.dma_start(xn[:, t, :], x_t[:, t, :]).then_inc(x_loaded[t], 16)
            sp.dma_start(fw_raw[:, :, :], fw.rearrange("(o p) h -> p o h", p=P)).then_inc(fw_loaded, 16)
            for c in range(KC):
                if c >= 2:
                    sp.wait_ge(w_lo_ready, c - 1)
                sp.dma_start(w_stage[:, c % 2, :], w_c[:, c, :]).then_inc(w_loaded[c], 16)

            def load_stack(i, j):
                rows = slice(HD * j, HD * j + HD)
                for stack, parts in ((q_stack, (q_hi, q_hi, q_lo, q_lo)), (k_stack, (k_hi, k_lo, k_hi, k_lo))):
                    for r, part in enumerate(parts):
                        sp.dma_start(stack[HD * r:HD * r + HD, j, :].bitcast(F32),
                                     part[rows, bass.ds(i, 1), :].rearrange("p a s -> p (a s)").bitcast(F32),
                                     ).then_inc(stack_loaded[j], 16)

            def load_shift(j, wait):
                sp.wait_ge(shift_copied, wait)
                sp.dma_start(q_stack[ROW_SHIFT:ROW_SHIFT + 2, j, :].rearrange("r (t q) -> r t q", t=TB).bitcast(F32),
                             shift_row[:, j % HALF, :]).then_inc(shift_loaded[j], 16)

            def compact(i, half):
                sp.wait_ge(ctx_evacuated, 2 * i + half + 1)
                if half == 0:
                    sp.wait_ge(ctx_divided, i)
                for h in range(HALF):
                    r = slice(HALF * HD * half + HD * h, HALF * HD * half + HD * h + HD)
                    sp.dma_start(ctx_c[r, :], ctx_raw[32 * h:32 * h + HD, half, :]).then_inc(compact_loaded[half], 16)
                    sp.dma_start(den_c[r, :], ctx_raw[32 * h + HD:32 * h + 2 * HD, half, :]).then_inc(compact_loaded[half], 16)

            def step(i, j, first=False, last=False):
                if not (last and j + 2 >= OCT):
                    load_shift((j + 2) % OCT, OCT * i + j + 3)
                if not last:
                    sp.wait_ge(scores_ready, TB * OCT * i + TB * (j + 1))
                    load_stack(i + 1, j)
                if j == 3 and not first:
                    compact(i - 1, 1)
                if j == 7:
                    compact(i, 0)

            sp.wait_ge(gate_ready, T)
            sp.wait_ge(w_lo_ready, KC)
            sp.wait_ge(job_evacuated, JOB_QK + 2)
            for j in range(6):
                load_stack(0, j)
            sp.wait_ge(job_ready, JOBS)
            for j in range(6, OCT):
                load_stack(0, j)
            load_shift(0, 1)
            load_shift(1, 2)
            sp.wait_ge(job_evacuated, JOBS)
            sp.dma_start(ow_raw[:, :, :], ow.rearrange("(c p) n -> p c n", p=P)).then_inc(late_loaded, 16)
            sp.dma_start(row_bias[:, :], ob.partition_broadcast(P)).then_inc(late_loaded, 16)
            sp.dma_start(x_res[:, :, :], x_t).then_inc(late_loaded, 16)
            for j in range(OCT):
                step(0, j, first=True)
            with sp.Fori(1, GROUPS - 1) as i:
                for j in range(OCT):
                    step(i, j)
            for j in range(OCT):
                step(GROUPS - 1, j, last=True)
            compact(GROUPS - 1, 1)
            for t in range(T):
                sp.wait_ge(out_ready, t + 1)
                sp.dma_start(out_t[:, t, :], x_res[:, t, :]).then_inc(out_stored, 16)
            sp.wait_ge(out_stored, 16 * T)

        @block.tensor
        def _(pe):
            def begin(job):
                if job >= BANKS:
                    pe.wait_ge(job_evacuated, job - BANKS + 1)
                return bank[job % BANKS]

            def product(dst, stationary, moving):
                terms = [(0, 1), (1, 0), (0, 0)]
                n = 0
                for a, b in terms:
                    for c in range(KC):
                        mm = pe.matmul(dst, stationary(a, c), moving(b, c), start=(n == 0), stop=(n == 3 * KC - 1))
                        n += 1
                return mm

            xt, fwt, centt, w, oww = (xt_hi, xt_lo), (fwt_hi, fwt_lo), (centt_hi, centt_lo), (w_hi, w_lo), (ow_hi, ow_lo)
            ctxs = (ctx_hi, ctx_lo)

            pe.wait_ge(consts_ready, 1)
            for b in range(B):
                pe.wait_ge(xn_ready, TB * (b + 1))
                for c in range(KC):
                    dst = begin(JOB_XT + KC * b + c)
                    for t in range(TB):
                        mm = pe.transpose(dst[:, t * P:(t + 1) * P], xn[:, TB * b + t, c * P:(c + 1) * P], ident[:, :])
                    mm.then_inc(job_ready, 1)
            pe.wait_ge(fw_loaded, 16)
            for c in range(KC):
                dst = begin(JOB_WT + c)
                for o in range(N // P):
                    mm = pe.transpose(dst[:, o * P:(o + 1) * P], fw_raw[:, o, c * P:(c + 1) * P], ident[:, :])
                mm.then_inc(job_ready, 1)
            pe.wait_ge(cent_loaded, 32)
            dst = begin(JOB_CENT)
            for c in range(KC):
                pe.transpose(dst[:, c * CL:(c + 1) * CL], cent_raw[:, c * P:(c + 1) * P], ident[0:CL, 0:CL])
            pe.transpose(dst[:, KC * CL:KC * CL + 2 * KC], qkb_raw[:, :], ident[0:2 * KC, 0:2 * KC]).then_inc(job_ready, 1)
            pe.wait_ge(job_evacuated, JOB_CENT + 1)
            dst = begin(JOB_LOGITS)
            for t in range(T):
                mm = product(dst[:, t * CL:(t + 1) * CL], lambda a, c: xt[a][:, c, t * P:(t + 1) * P],
                             lambda b, c: centt[b][:, c, :])
            mm.then_inc(job_ready, 1)

            def dense(t):
                dst = begin(JOB_DENSE[t])
                product(dst, lambda a, c: xt[a][:, c, t * P:(t + 1) * P], lambda b, c: fwt[b][:, c, :]).then_inc(job_ready, 1)

            for t in range(3):
                dense(t)
            pe.wait_ge(hits_ready, 1)
            dst = begin(JOB_COUNT)
            for t in range(T):
                mm = pe.matmul(dst[0:CL, 0:P], hits[:, t, :], ones_bf[:, :], start=(t == 0), stop=(t == T - 1))
            mm.then_inc(job_ready, 1)
            dense(3)
            pe.wait_ge(onehot_ready, 1)
            pe.wait_ge(job_evacuated, JOB_COUNT + 1)
            pe.matmul(begin(JOB_ROWSEL), cl_sel[:, :], onehot[:, :], start=True, stop=True).then_inc(job_ready, 1)
            for t in range(4, T):
                dense(t)
            pe.wait_ge(w_lo_ready, KC)
            for n, (g, which) in enumerate(qk_jobs):
                b, o = g // OPB, g % OPB
                col = which * H + o * P
                dst = begin(JOB_QK + n)
                product(dst, lambda a, c: w[a][:, c, col:col + P],
                        lambda m, c: xt[m][:, c, b * S:(b + 1) * S]).then_inc(job_ready, 1)
            for t in range(T):
                dst = begin(JOB_V + t)
                product(dst, lambda a, c: xt[a][:, c, t * P:(t + 1) * P],
                        lambda m, c: w[m][:, c, 2 * H:3 * H]).then_inc(job_ready, 1)

            def max_scores(i, j, first=False):
                pe.wait_ge(stack_loaded[j], LOAD * i + LOAD)
                for u in range(2):
                    if first and j == 0:
                        pe.wait_ge(job_evacuated, JOB_V + 2 * u + 2)
                    else:
                        pe.wait_ge(maxes_ready, 2 * OCT * i + 2 * j + u - 1)
                    for v in range(2):
                        q = (2 * u + v) * P
                        mm = pe.matmul(max_tile[u][:, v, :], q_stack[0:ROWS_MAX, j, q:q + P], k_stack[0:ROWS_MAX, j, :],
                                       start=True, stop=True)
                    mm.then_inc(max_scores_ready, 1)

            def turn_shift(j, split):
                pe.wait_ge(shift_split, split)
                pe.wait_ge(shift_copied, split - 1)
                pe.matmul(turn_bank[0:2 * TB, 0:P], shift[:, j, :], ident[:, :], start=True, stop=True).then_inc(shift_turned, 1)

            def context(i, half, kt):
                if kt == 0:
                    pe.wait_ge(probs_ready, 2 * TB * HALF * i + TB * HALF * (half + 1))
                    pe.wait_ge(v_ready, 2 * i + half + 1)
                    pe.wait_ge(ctx_evacuated, 2 * i + half)
                for h in range(HALF):
                    a, b = (h, kt) if half == 0 else (kt, h)
                    mm = pe.matmul(ctx_bank[32 * h:32 * h + 32, :], v_ring[:, half, kt, h, :], probs[:, a, b, :],
                                   start=(kt == 0), stop=(kt == TB - 1))
                mm.then_inc(probs_used, 1)

            def scores(i, j, first):
                pe.wait_ge(shift_loaded[j], 16 * i + 16)
                for kt in range(TB):
                    if not (first and j == 0 and kt < 2):
                        pe.wait_ge(probs_ready, TB * OCT * i + TB * j + kt - 1)
                    pe.matmul(exp_tile[kt % 2], k_stack[0:ROWS_EXP, j, kt * P:(kt + 1) * P], q_stack[0:ROWS_EXP, j, :],
                              start=True, stop=True).then_inc(scores_ready, 1)

            def step(i, j, first=False, last=False):
                if not (last and j >= 4):
                    max_scores(i if j < 4 else i + 1, (j + 4) % OCT)
                if j >= 4:
                    context(i, 0, j - 4)
                elif not first:
                    context(i - 1, 1, j)
                if not (last and j + 2 >= OCT):
                    turn_shift((j + 2) % OCT, OCT * i + j + 3)
                scores(i, j, first)

            pe.wait_ge(pads_ready, 1)
            for j in range(4):
                max_scores(0, j, first=True)
            pe.wait_ge(job_evacuated, JOBS)
            turn_shift(0, 1)
            turn_shift(1, 2)
            pe.wait_ge(pads_ready, 3)
            for j in range(OCT):
                step(0, j, first=True)
            with pe.Fori(1, GROUPS - 1) as i:
                for j in range(OCT):
                    step(i, j)
            for j in range(OCT):
                step(GROUPS - 1, j, last=True)
            for kt in range(TB):
                context(GROUPS - 1, 1, kt)

            pe.wait_ge(maxes_ready, 2 * OCT * GROUPS)
            pe.wait_ge(ow_ready, 1)
            for t in range(T):
                b, q = t // TB, (t % TB) * P
                if t % TB == 0:
                    pe.wait_ge(ctx_split, OPB * (b + 1))
                if t == 4:
                    pe.wait_ge(probs_ready, TB * OCT * GROUPS)
                if t == 6:
                    pe.wait_ge(shift_copied, OCT * GROUPS)
                if t == 7:
                    pe.wait_ge(ctx_evacuated, 2 * GROUPS)
                product(out_bank[t], lambda a, c: ctxs[a][:, OPB * b + c, q:q + P],
                        lambda m, c: oww[m][:, c, :]).then_inc(out_tile_ready, 1)

        @block.scalar
        def _(act):
            act.dma_start(cent_raw[:, :], cent).then_inc(cent_loaded, 16)
            act.dma_start(qkb_raw[:, :], qkvb[0:2 * H].rearrange("(c p) -> c p", p=P)).then_inc(cent_loaded, 16)
            act.dma_start(assign_b[:, :], assign.partition_broadcast(CL)).then_inc(small_loaded, 16)
            act.dma_start(fb_b[:, :], fb.partition_broadcast(P)).then_inc(small_loaded, 16)
            act.dma_start(row_bias[:, :], qkvb[2 * H:3 * H].partition_broadcast(P)).then_inc(small_loaded, 16)

            for n in range(SPLITS_A):
                act.wait_ge(job_ready, n + 1)
                if n < JOB_WT:
                    b, c = n // KC, n % KC
                    dst, src = xt_hi[:, c, b * S:(b + 1) * S], bank[n % BANKS]
                elif n < JOB_CENT:
                    dst, src = fwt_hi[:, n - JOB_WT, :], bank[n % BANKS]
                else:
                    dst, src = centt_hi[:, :, :].rearrange("p c k -> p (c k)"), bank[n % BANKS][:, 0:KC * CL]
                nc.scalar.copy(dst, src).then_inc(hi_ready, 1)
            act.wait_ge(job_evacuated, JOB_LOGITS + 1)
            nc.scalar.activation(expo[:, :, :], logit[:, :, :], ACT.Exp, scale=SHARP).then_inc(exp_ready, 1)
            for c in range(KC):
                act.wait_ge(w_loaded[c], 16)
                nc.scalar.copy(w_hi[:, c, :], w_stage[:, c % 2, :]).then_inc(w_hi_ready, 1)
            for t in range(T):
                act.wait_ge(masked_ready, t + 1)
                nc.scalar.activation(gate_exp[:, t, :], gate[:, t, :], ACT.Exp, scale=-1.0).then_inc(gate_exp_ready, 1)
            for n, (g, which) in enumerate(qk_jobs):
                act.wait_ge(job_ready, JOB_QK + n + 1)
                col = which * KC + g % OPB
                nc.scalar.activation((q_hi, k_hi)[which][:, g, :], bank[(JOB_QK + n) % BANKS], ACT.Identity,
                                     bias=qkb[:, col:col + 1]).then_inc(hi_ready, 1)

            def copy_shift(j, turned, loaded):
                act.wait_ge(shift_turned, turned)
                if loaded is not None:
                    act.wait_ge(shift_loaded[(j + HALF) % OCT], loaded)
                nc.scalar.copy(shift_row[:, j % HALF, :], turn_bank[0:2 * TB, 0:P]).then_inc(shift_copied, 1)

            def evacuate(i, half):
                act.wait_ge(probs_used, 2 * TB * i + TB * (half + 1))
                act.wait_ge(compact_loaded[half], LOAD * i)
                nc.scalar.copy(ctx_raw[:, half, :], ctx_bank).then_inc(ctx_evacuated, 1)

            def step(i, j, first=False, last=False):
                if j == 7:
                    evacuate(i, 0)
                if j == 3 and not first:
                    evacuate(i - 1, 1)
                if not (last and j + 2 >= OCT):
                    copy_shift((j + 2) % OCT, OCT * i + j + 3, 16 * i if j < 2 else 16 * i + 16)
                for kt in range(TB):
                    act.wait_ge(scores_ready, TB * OCT * i + TB * j + kt + 1)
                    a, b = (j, kt) if j < HALF else (kt, j - HALF)
                    nc.scalar.activation(probs[:, a, b, :], exp_tile[kt % 2], ACT.Exp, scale=SCALE).then_inc(probs_ready, 1)

            copy_shift(0, 1, None)
            copy_shift(1, 2, None)
            for j in range(OCT):
                step(0, j, first=True)
            for j in range(OCT):
                step(1, j)
            with act.Fori(2, GROUPS - 1) as i:
                for j in range(OCT):
                    step(i, j)
            for j in range(OCT):
                step(GROUPS - 1, j, last=True)
            evacuate(GROUPS - 1, 1)

        @block.vector
        def _(dve):
            steps = [0]

            def link(ins):
                steps[0] += 1
                ins.then_inc(dve_step, 1)
                dve.wait_ge(dve_step, steps[0])

            for b in range(B):
                tiles = range(TB * b, TB * (b + 1))
                for t in tiles:
                    dve.wait_ge(x_loaded[t], 16)
                    nc.vector.bn_stats(stats[:, t, :], xn[:, t, :]).then_inc(stats_done, 1)
                for t in tiles:
                    dve.wait_ge(stats_done, t + 1)
                    nc.vector.bn_aggr(mv[:, t, :], stats[:, t, :]).then_inc(aggr_done, 1)
                dve.wait_ge(aggr_done, TB * (b + 1))
                nc.vector.tensor_scalar_add(var_eps[:, TB * b:TB * (b + 1)], mv[:, TB * b:TB * (b + 1), 1], EPS).then_inc(var_ready, 1)
                dve.wait_ge(rstd_ready, b + 1)
                for t in tiles:
                    nc.vector.tensor_scalar(xn[:, t, :], xn[:, t, :], mv[:, t, 0:1], rstd[:, t:t + 1],
                                            ALU.subtract, ALU.mult).then_inc(xn_ready, 1)

            def evacuated(ins):
                ins.then_inc(job_evacuated, 1)

            for n in range(SPLITS_A):
                dve.wait_ge(hi_ready, n + 1)
                src = bank[n % BANKS]
                if n < JOB_WT:
                    b, c = n // KC, n % KC
                    hi, lo = xt_hi[:, c, b * S:(b + 1) * S], xt_lo[:, c, b * S:(b + 1) * S]
                elif n < JOB_CENT:
                    hi, lo = fwt_hi[:, n - JOB_WT, :], fwt_lo[:, n - JOB_WT, :]
                else:
                    link(nc.vector.tensor_copy(qkb[:, :], src[:, KC * CL:KC * CL + 2 * KC]))
                    src = src[:, 0:KC * CL]
                    hi, lo = (h[:, :, :].rearrange("p c k -> p (c k)") for h in (centt_hi, centt_lo))
                evacuated(nc.vector.tensor_tensor(lo, src, hi.bitcast(F32), ALU.subtract))

            dve.wait_ge(iota_ready, 1)
            link(nc.vector.tensor_copy(iota_f[:, :], iota_i[:, :]))
            dve.wait_ge(small_loaded, 48)
            nc.vector.tensor_scalar(onehot[:, :], assign_b[:, :], iota_f[:, 0:1], None, ALU.is_equal).then_inc(onehot_ready, 1)

            dve.wait_ge(job_ready, JOB_LOGITS + 1)
            lg = bank[JOB_LOGITS % BANKS].rearrange("p (t k) -> p t k", t=T)
            link(nc.vector.tensor_reduce(lmax[:, :], lg, AX.X, ALU.max))
            evacuated(nc.vector.tensor_tensor(logit[:, :, :], lg, lmax[:, :].unsqueeze(2).to_broadcast([P, T, CL]), ALU.subtract))

            def evacuate_dense(t):
                dve.wait_ge(job_ready, JOB_DENSE[t] + 1)
                evacuated(nc.vector.tensor_tensor(gate[:, t, :], bank[JOB_DENSE[t] % BANKS], fb_b[:, :], ALU.add))

            def mask(t):
                nc.vector.scalar_tensor_tensor(gate[:, t, :], gate[:, t, :], q_sel[:, t:t + 1], row_sel[:, :],
                                               ALU.mult, ALU.mult).then_inc(masked_ready, 1)

            evacuate_dense(0)
            dve.wait_ge(exp_ready, 1)
            link(nc.vector.tensor_reduce(thr[:, :], expo[:, :, :], AX.X, ALU.add))
            link(nc.vector.tensor_scalar(thr[:, :], thr[:, :], HIT, None, ALU.mult))
            nc.vector.tensor_tensor(hits[:, :, :], expo[:, :, :], thr[:, :].unsqueeze(2).to_broadcast([P, T, CL]),
                                    ALU.is_gt).then_inc(hits_ready, 1)
            dve.wait_ge(hits_ready, 1)
            link(nc.vector.tensor_reduce(q_sel[:, :], hits[:, :, :], AX.X, ALU.max))
            evacuate_dense(1)
            evacuate_dense(2)
            dve.wait_ge(job_ready, JOB_COUNT + 1)
            evacuated(nc.vector.tensor_scalar(cl_sel[:, :], bank[JOB_COUNT % BANKS][0:CL, 0:P], 0.5, None, ALU.is_gt))
            evacuate_dense(3)
            dve.wait_ge(job_ready, JOB_ROWSEL + 1)
            evacuated(nc.vector.tensor_copy(row_sel[:, :], bank[JOB_ROWSEL % BANKS]))
            dve.wait_ge(job_evacuated, JOB_ROWSEL + 1)
            for t in range(4):
                mask(t)
            for t in range(4, T):
                evacuate_dense(t)
                dve.wait_ge(job_evacuated, JOB_DENSE[t] + 1)
                mask(t)

            for n, (g, which) in enumerate(qk_jobs):
                dve.wait_ge(hi_ready, SPLITS_A + n + 1)
                col = which * KC + g % OPB
                evacuated(nc.vector.scalar_tensor_tensor(
                    (q_lo, k_lo)[which][:, g, :], bank[(JOB_QK + n) % BANKS], qkb[:, col:col + 1],
                    (q_hi, k_hi)[which][:, g, :].bitcast(F32), ALU.add, ALU.subtract))
                if n % 2:
                    dve.wait_ge(gate_den_ready, n // 2 + 1)
                    nc.vector.reciprocal(gate_exp[:, n // 2, :], gate_exp[:, n // 2, :]).then_inc(gate_inverted, 1)
            dve.wait_ge(gate_ready, T)
            for t in range(T):
                b, kt = t // TB, t % TB
                dve.wait_ge(job_ready, JOB_V + t + 1)
                evacuated(nc.vector.tensor_tensor(
                    v_all[:, b * OPB:(b + 1) * OPB, kt, :], bank[(JOB_V + t) % BANKS].rearrange("p (o c) -> p o c", o=OPB),
                    row_bias[:, :].rearrange("p (o c) -> p o c", o=OPB), ALU.add))

            def invert(i):
                dve.wait_ge(compact_loaded[0], LOAD * i + LOAD)
                dve.wait_ge(compact_loaded[1], LOAD * i + LOAD)
                nc.vector.reciprocal(den_c[:, :], den_c[:, :]).then_inc(den_inverted, 1)

            def maxima(i, first=False, octets=False):
                for j in range(OCT):
                    if octets and j == 1:
                        invert(i - 2)
                    if not first:
                        dve.wait_ge(shift_split, OCT * i + j + 1 - OCT)
                    for u in range(2):
                        dve.wait_ge(max_scores_ready, 2 * OCT * i + 2 * j + u + 1)
                        nc.vector.tensor_reduce(neg_max[:, j, 2 * u:2 * u + 2], max_tile[u][:, :, :], AX.X, ALU.max,
                                                negate=True).then_inc(maxes_ready, 1)

            maxima(0, first=True)
            maxima(1)
            with dve.Fori(2, GROUPS) as i:
                maxima(i, octets=True)
            invert(GROUPS - 2)

            dve.wait_ge(late_loaded, 48)
            dve.wait_ge(v_ready, 2 * GROUPS)
            link(nc.vector.tensor_copy(ow_hi[:, :, :], ow_raw[:, :, :]))
            nc.vector.tensor_tensor(ow_lo[:, :, :], ow_raw[:, :, :], ow_hi[:, :, :].bitcast(F32), ALU.subtract).then_inc(ow_ready, 1)
            for t in range(T):
                link(nc.vector.tensor_tensor(ob_gate[:, :], row_bias[:, :], gate[:, t, :], ALU.mult))
                link(nc.vector.tensor_tensor(x_res[:, t, :], x_res[:, t, :], ob_gate[:, :], ALU.add))
            invert(GROUPS - 1)
            for t in range(T):
                dve.wait_ge(out_tile_ready, t + 1)
                nc.vector.tensor_tensor(gate[:, t, :], out_bank[t], gate[:, t, :], ALU.mult).then_inc(gated_ready, 1)
                dve.wait_ge(gated_ready, t + 1)
                nc.vector.tensor_tensor(x_res[:, t, :], x_res[:, t, :], gate[:, t, :], ALU.add).then_inc(out_ready, 1)

        @block.gpsimd
        def _(pool):
            steps = [0]

            def link(ins):
                steps[0] += 1
                ins.then_inc(pool_step, 1)
                pool.wait_ge(pool_step, steps[0])

            nc.gpsimd.memset(neg_half[:, :], -0.5)
            nc.gpsimd.memset(zeros[:, :], 0.0)
            link(nc.gpsimd.memset(ident[:, :], 0.0))
            nc.gpsimd.affine_select(out=ident[:, :], in_=ident[:, :], compare_op=ALU.not_equal, fill=1.0, base=0,
                                    pattern=[[-1, P]], channel_multiplier=1).then_inc(consts_ready, 1)
            nc.gpsimd.iota(iota_i[:, :], [[0, 1]], base=0, channel_multiplier=1).then_inc(iota_ready, 1)
            link(nc.gpsimd.memset(ones_bf[:, :], 1.0))
            for b in range(B):
                pool.wait_ge(var_ready, b + 1)
                r = slice(TB * b, TB * (b + 1))
                nc.gpsimd.tensor_tensor(rstd[:, r], var_eps[:, r], neg_half[:, r], ALU.pow).then_inc(rstd_ready, 1)
            for c in range(KC):
                pool.wait_ge(w_hi_ready, c + 1)
                nc.gpsimd.tensor_tensor(w_lo[:, c, :], w_stage[:, c % 2, :], w_hi[:, c, :].bitcast(F32),
                                        ALU.subtract).then_inc(w_lo_ready, 1)
            for t in range(T):
                pool.wait_ge(gate_exp_ready, t + 1)
                nc.gpsimd.tensor_scalar(gate_exp[:, t, :], gate_exp[:, t, :], 1.0, None, ALU.add).then_inc(gate_den_ready, 1)
            for t in range(T):
                pool.wait_ge(gate_inverted, t + 1)
                nc.gpsimd.tensor_tensor(gate[:, t, :], gate[:, t, :], gate_exp[:, t, :], ALU.mult).then_inc(gate_ready, 1)
            pool.wait_ge(gate_ready, T)
            pool.wait_ge(w_lo_ready, KC)
            early = 6
            link(nc.gpsimd.memset(q_stack[64:ROWS_MAX, :, :].bitcast(F32), 0.0))
            link(nc.gpsimd.memset(k_stack[64:ROWS_MAX, 0:early, :].bitcast(F32), 0.0))
            nc.gpsimd.memset(k_stack[ROW_SHIFT:ROWS_EXP, 0:early, :].bitcast(F32), 1.0).then_inc(pads_ready, 1)
            pool.wait_ge(pads_ready, 1)
            pool.wait_ge(job_ready, JOBS)
            nc.gpsimd.memset(k_stack[64:ROWS_MAX, early:OCT, :].bitcast(F32), 0.0).then_inc(pads_ready, 1)
            pool.wait_ge(pads_ready, 2)
            nc.gpsimd.memset(k_stack[ROW_SHIFT:ROWS_EXP, early:OCT, :].bitcast(F32), 1.0).then_inc(pads_ready, 1)
            pool.wait_ge(pads_ready, 3)
            link(nc.gpsimd.memset(v_ring[:, :, :, :, HD:2 * HD], 1.0))

            def split_shift(i, j, first=False):
                pool.wait_ge(maxes_ready, 2 * OCT * i + 2 * j + 2)
                if not first:
                    pool.wait_ge(shift_turned, OCT * i + j + 1 - OCT)
                nc.gpsimd.tensor_tensor(shift[:, j, 0:TB].bitcast(F32R), neg_max[:, j, :], zeros[:, :], ALU.add).then_inc(shift_hi_ready, 1)
                pool.wait_ge(shift_hi_ready, OCT * i + j + 1)
                nc.gpsimd.tensor_tensor(shift[:, j, TB:2 * TB], neg_max[:, j, :], shift[:, j, 0:TB],
                                        ALU.subtract).then_inc(shift_split, 1)

            def group(buffer, i):
                return buffer[:, bass.ds(i, 1), :].rearrange("p a s -> p (a s)")

            def fill_v(i, half, first=False):
                if not first:
                    pool.wait_ge(probs_used, 2 * TB * i + TB * half - TB)
                cols = slice(HALF * HD * half, HALF * HD * (half + 1))
                nc.gpsimd.tensor_copy(
                    v_ring[:, half, :, :, 0:HD],
                    v_all[:, bass.ds(i, 1), :, cols].rearrange("p a t (h d) -> p (a t) h d", d=HD)).then_inc(v_ready, 1)

            def divide(i):
                pool.wait_ge(den_inverted, i + 1)
                nc.gpsimd.tensor_tensor(ctx_n[:, :], ctx_c[:, :], den_c[:, :], ALU.mult).then_inc(ctx_divided, 1)

            def context_hi(i):
                pool.wait_ge(ctx_divided, i + 1)
                nc.gpsimd.tensor_copy(group(ctx_hi, i), ctx_n[:, :]).then_inc(ctx_hi_ready, 1)

            def context_lo(i):
                pool.wait_ge(ctx_hi_ready, i + 1)
                nc.gpsimd.tensor_tensor(group(ctx_lo, i), ctx_n[:, :], group(ctx_hi, i).bitcast(F32),
                                        ALU.subtract).then_inc(ctx_split, 1)
                pool.wait_ge(ctx_split, i + 1)

            def steps_of(i, octets=True, first=False):
                for j in range(OCT):
                    split_shift(i, j, first)
                    if j == 0 and not first:
                        fill_v(i - 1, 1)
                    if j == 4:
                        fill_v(i, 0, first)
                    if octets and j == 0:
                        divide(i - 2)
                    if octets and j == 2:
                        context_hi(i - 2)
                    if octets and j == 3:
                        context_lo(i - 2)

            steps_of(0, octets=False, first=True)
            steps_of(1, octets=False)
            with pool.Fori(2, GROUPS) as i:
                steps_of(i)
            fill_v(GROUPS - 1, 1)
            for g in range(GROUPS - 2, GROUPS):
                divide(g)
                context_hi(g)
                context_lo(g)


_INS = ["L0_attn_x", "L0_attn_attn_qkvw", "L0_attn_attn_qkvb", "L0_attn_attn_ow", "L0_attn_attn_ob",
        "L0_ffn_weight", "L0_ffn_bias", "L0_ffn_centroids", "L0_ffn_assignments"]


def kernel(**inputs):
    import numpy as _np
    import concourse.bacc as _bacc
    from concourse import mybir as _mybir
    from concourse.bass_utils import run_bass_kernel_spmd as _run

    nc = _bacc.Bacc("TRN2", target_bir_lowering=False, num_devices=1)
    arrays, args = {}, []
    for name in _INS:
        a = _np.ascontiguousarray(inputs[name])
        arrays[f"in_{name}"] = a
        args.append(nc.dram_tensor(f"in_{name}", a.shape, _mybir.dt.from_np(a.dtype), kind="ExternalInput").ap())
    shape = arrays["in_L0_attn_x"].shape
    out = nc.dram_tensor("out_x", shape, _mybir.dt.float32, kind="ExternalOutput").ap()
    build(nc, *args, out)
    r = _run(nc, [arrays], core_ids=[0])
    return r.results[0]["out_x"]
```

```python
from contextlib import ExitStack

import concourse.bass as bass
from concourse import mybir

F32 = mybir.dt.float32
F32R = mybir.dt.float32r
BF16 = mybir.dt.bfloat16
I32 = mybir.dt.int32
ALU = mybir.AluOpType
ACT = mybir.ActivationFunctionType
AX = mybir.AxisListType

P = 128
BANK = 512
BANKS = 8


def build(nc, x, qkvw, qkvb, ow, ob, fw, fb, cent, assign, out):
    B, S, H = x.shape
    N = fw.shape[0]
    CL = cent.shape[0]
    HD = 16
    HEADS = H // HD
    T = B * S // P
    TB = S // P
    KC = H // P
    OCT = P // HD
    GROUPS = B * HEADS // OCT
    OPB = GROUPS // B
    HALF = OCT // 2
    EPS = 1e-5
    SHARP = 10.0
    HIT = 0.01
    SCALE = HD ** -0.5
    ROWS_MAX, ROW_SHIFT, ROWS_EXP = 96, 96, 98
    BODY = 2 * OCT
    TURNS = B * HEADS // BODY
    QUADS = BODY // HALF
    LOAD = 6 * 16
    PACK = (HALF + 1) * 16
    assert S == BANK and N == BANK and H == 4 * P and T == 8 and KC == TB == 4 and CL == 64

    x_t = x.rearrange("b (t p) h -> p (b t) h", p=P)
    out_t = out.rearrange("b (t p) h -> p (b t) h", p=P)
    w_c = qkvw.rearrange("(c p) n -> p c n", p=P)

    JOB_XT, JOB_WT, JOB_CENT, JOB_LOGITS = 0, 8, 12, 13
    JOB_DENSE = [14, 15, 16, 18, 20, 21, 22, 23]
    JOB_COUNT, JOB_ROWSEL, JOB_QK, JOB_V = 17, 19, 24, 40
    JOBS = 48
    SPLITS_A = 13
    qk_jobs = [(g, which) for g in range(GROUPS) for which in range(2)]

    parts_dram = nc.dram_tensor("qk_parts", [2, B * HEADS, 2, HD, S], F32, kind="Internal").ap()

    with ExitStack() as ctx:
        def sem(name):
            return ctx.enter_context(nc.semaphore(name))

        def sems(name, n):
            return [sem(f"{name}{i}") for i in range(n)]

        start = (nc.sbuf_base + 63) // 64 * 64
        KB = 1024

        def at(name, offset, shape, dt):
            return nc.alloc_sbuf_tensor_at(name, shape, dt, offset=start + offset)

        QK, V, G, X, STAGE, WHI, WLO, XT, ROW, SMALL = (n * KB for n in (0, 64, 80, 96, 112, 124, 148, 172, 204, 206))
        q_hi = at("q_hi", QK, [P, GROUPS, S], F32R)
        q_lo = at("q_lo", QK + 16 * KB, [P, GROUPS, S], F32R)
        k_hi = at("k_hi", QK + 32 * KB, [P, GROUPS, S], F32R)
        k_lo = at("k_lo", QK + 48 * KB, [P, GROUPS, S], F32R)
        v_all = at("v_all", V, [P, GROUPS, TB, P], F32)
        gate = at("gate", G, [P, T, N], F32)
        xn = at("xn", X, [P, T, H], F32)
        gate_exp = at("gate_exp", X, [P, T, N], F32)
        w_stage = at("w_stage", STAGE, [P, 2, 3 * H], F32)
        w_hi = at("w_hi", WHI, [P, KC, 3 * H], F32R)
        w_lo = at("w_lo", WLO, [P, KC, 3 * H], F32R)
        xt_hi = at("xt_hi", XT, [P, KC, T * P], F32R)
        xt_lo = at("xt_lo", XT + 16 * KB, [P, KC, T * P], F32R)
        fw_raw = at("fw_raw", QK, [P, KC, H], F32)
        fwt_hi = at("fwt_hi", QK + 8 * KB, [P, KC, N], F32R)
        fwt_lo = at("fwt_lo", QK + 16 * KB, [P, KC, N], F32R)
        cent_raw = at("cent_raw", QK + 24 * KB, [CL, H], F32)
        centt_hi = at("centt_hi", QK + 26 * KB, [P, KC, CL], F32R)
        centt_lo = at("centt_lo", QK + 27 * KB, [P, KC, CL], F32R)
        qkb_raw = at("qkb_raw", QK + 28 * KB, [2 * KC, P], F32)
        logit = at("logit", V, [P, T, CL], F32)
        expo = at("expo", V + 2 * KB, [P, T, CL], F32)
        hits = at("hits", V + 4 * KB, [P, T, CL], BF16)
        onehot = at("onehot", V + 5 * KB, [CL, N], BF16)
        assign_b = at("assign_b", V + 6 * KB, [CL, N], I32)
        row_sel = at("row_sel", V + 8 * KB, [P, N], F32)
        fb_b = at("fb_b", V + 10 * KB, [P, N], F32)
        ident = at("ident", SMALL, [P, P], F32)
        row_bias = at("row_bias", ROW, [P, N], F32)
        small = SMALL + 512
        ones_bf = at("ones_bf", small, [P, P], BF16)
        cl_sel = at("cl_sel", small + 256, [CL, P], BF16)
        stats = at("stats", small + 512, [P, T, 6], F32)
        mv = at("mv", small + 704, [P, T, 2], F32)
        var_eps = at("var_eps", small + 768, [P, T], F32)
        rstd = at("rstd", small + 800, [P, T], F32)
        neg_half = at("neg_half", small + 832, [P, T], F32)
        qkb = at("qkb", small + 864, [P, 2 * KC], F32)
        lmax = at("lmax", small + 896, [P, T], F32)
        thr = at("thr", small + 928, [P, T], F32)
        q_sel = at("q_sel", small + 960, [P, T], F32)
        zeros = at("zeros", small + 1056, [P, TB], F32)
        iota_i = at("iota_i", small + 992, [CL, 1], I32)
        iota_f = at("iota_f", small + 1024, [CL, 1], F32)
        shift = at("shift", small, [P, OCT, 2 * TB], F32)
        neg_max = at("neg_max", small + 512, [P, OCT, TB], F32)
        BUF = STAGE + 16 * KB
        q_stack = [at("q_stack0", X, [P, OCT, S], F32R), at("q_stack1", BUF, [P, OCT, S], F32R)]
        k_stack = [at("k_stack0", STAGE, [P, OCT, S], F32R), at("k_stack1", BUF + 16 * KB, [P, OCT, S], F32R)]
        probs = at("probs", BUF + 32 * KB, [P, HALF, HALF, S], F32)
        v_ring = at("v_ring", BUF + 64 * KB, [P, 2, TB, HALF, 2 * HD], F32)
        ctx_raw = at("ctx_raw", BUF + 68 * KB, [P, S], F32)
        ctx_c = at("ctx_c", BUF + 70 * KB, [P, S], F32)
        den_c = at("den_c", BUF + 72 * KB, [P, S], F32)
        ctx_n = at("ctx_n", BUF + 74 * KB, [P, S], F32)
        shift_row = at("shift_row", ROW, [2 * TB, HALF, P], F32)
        x_res = at("x_res", QK + 32 * KB, [P, T, H], F32)
        ow_raw = at("ow_raw", QK + 48 * KB, [P, KC, H], F32)
        ob_b = at("ob_b", QK + 56 * KB, [P, H], F32)
        ob_gate = at("ob_gate", QK + 58 * KB, [P, H], F32)
        ow_hi = at("ow_hi", V, [P, KC, H], F32R)
        ow_lo = at("ow_lo", V + 8 * KB, [P, KC, H], F32R)
        ctx_hi, ctx_lo = q_hi, q_lo

        pairs = [ctx.enter_context(nc.psum_tensor(f"banks{2 * i}", [P, 2, BANK], F32)) for i in range(4)]
        bank = [pairs[i // 2][:, i % 2, :] for i in range(BANKS)]
        max_tile = [pairs[0], pairs[1]]
        exp_tile = [bank[4], bank[5]]
        ctx_bank, turn_bank = bank[6], bank[7]
        out_bank = [bank[i] for i in (0, 1, 2, 3, 4, 5, 7, 6)]

        x_loaded = sems("x_loaded", T)
        fw_loaded, cent_loaded, small_loaded = sem("fw_loaded"), sem("cent_loaded"), sem("small_loaded")
        w_loaded = sems("w_loaded", KC)
        consts_ready, iota_ready = sem("consts_ready"), sem("iota_ready")
        stats_done, aggr_done, var_ready, rstd_ready, xn_ready = (
            sem("stats_done"), sem("aggr_done"), sem("var_ready"), sem("rstd_ready"), sem("xn_ready"))
        onehot_ready = sem("onehot_ready")
        job_ready, hi_ready, job_evacuated = sem("job_ready"), sem("hi_ready"), sem("job_evacuated")
        dve_step, pool_step = sem("dve_step"), sem("pool_step")
        exp_ready, hits_ready = sem("exp_ready"), sem("hits_ready")
        w_hi_ready, w_lo_ready = sem("w_hi_ready"), sem("w_lo_ready")
        masked_ready, gate_exp_ready, gate_ready = sem("masked_ready"), sem("gate_exp_ready"), sem("gate_ready")
        pads_ready = sem("pads_ready")
        parts_stored = sems("parts_stored", 3)
        stack_loaded = sems("stack_loaded", 2)
        shift_loaded = sems("shift_loaded", OCT)
        max_scores_ready, maxes_ready, shift_split = sem("max_scores_ready"), sem("maxes_ready"), sem("shift_split")
        shift_turned, shift_copied = sem("shift_turned"), sem("shift_copied")
        scores_ready, probs_ready, probs_used = sem("scores_ready"), sem("probs_ready"), sem("probs_used")
        v_ready, ctx_evacuated = sem("v_ready"), sem("ctx_evacuated")
        compact_loaded = sems("compact_loaded", 2)
        gate_den_ready, gate_inverted, den_inverted = sem("gate_den_ready"), sem("gate_inverted"), sem("den_inverted")
        ctx_divided, ctx_hi_ready, ctx_split = sem("ctx_divided"), sem("ctx_hi_ready"), sem("ctx_split")
        shift_hi_ready = sem("shift_hi_ready")
        late_loaded = sem("late_loaded")
        ow_ready, rest_ready, rest_step = sem("ow_ready"), sem("rest_ready"), sem("rest_step")
        out_tile_ready, gated_ready, out_ready, out_stored = (
            sem("out_tile_ready"), sem("gated_ready"), sem("out_ready"), sem("out_stored"))

        block = ctx.enter_context(nc.Block())

        @block.sync
        def _(sp):
            for t in range(T):
                sp.dma_start(xn[:, t, :], x_t[:, t, :]).then_inc(x_loaded[t], 16)
            sp.dma_start(fw_raw[:, :, :], fw.rearrange("(o p) h -> p o h", p=P)).then_inc(fw_loaded, 16)
            for c in range(KC):
                if c >= 2:
                    sp.wait_ge(w_lo_ready, c - 1)
                sp.dma_start(w_stage[:, c % 2, :], w_c[:, c, :]).then_inc(w_loaded[c], 16)

            def store_parts(n):
                g, which = qk_jobs[n]
                sp.wait_ge(job_evacuated, JOB_QK + n + 1)
                for part, src in enumerate(((q_hi, q_lo), (k_hi, k_lo))[which]):
                    sp.dma_start(parts_dram[which, g * OCT:(g + 1) * OCT, part, :, :],
                                 src[:, g, :].bitcast(F32)).then_inc(parts_stored[min(g, 2)], 16)

            def load_stack(e, g):
                heads = parts_dram.rearrange("w (g j) x d s -> w (x d) g j s", j=OCT)
                for r in range(2):
                    sp.dma_start(q_stack[e][2 * HD * r:2 * HD * (r + 1), :, :].bitcast(F32),
                                 heads[0, :, bass.ds(g, 1), :, :].rearrange("r a j s -> r (a j) s")).then_inc(stack_loaded[e], 16)
                for r in range(4):
                    rows = slice(HD * (r // 2), HD * (r // 2) + HD)
                    sp.dma_start(k_stack[e][HD * r:HD * (r + 1), :, :].bitcast(F32),
                                 heads[1, rows, bass.ds(g, 1), :, :].rearrange("r a j s -> r (a j) s")).then_inc(stack_loaded[e], 16)

            def load_shift(j, copied):
                sp.wait_ge(shift_copied, copied)
                sp.dma_start(
                    q_stack[j // OCT][ROW_SHIFT:ROW_SHIFT + 2, j % OCT, :].rearrange("r (t q) -> r t q", t=TB).bitcast(F32),
                    shift_row[:, j % HALF, :]).then_inc(shift_loaded[j % OCT], 16)

            def compact(i, m):
                sp.wait_ge(ctx_evacuated, QUADS * i + m + 1)
                base = HALF * HD * (m % 2)
                for h in range(HALF):
                    sp.dma_start(ctx_c[base + HD * h:base + HD * (h + 1), :],
                                 ctx_raw[32 * h:32 * h + HD, :]).then_inc(compact_loaded[m % 2], 16)
                row = ctx_raw[HD:P:32, :]
                sp.dma_start(den_c[base:base + HALF * HD, :],
                             bass.AP(tensor=row.tensor, offset=row.offset, ap=[row.ap[0], [0, HD], [1, S]]),
                             ).then_inc(compact_loaded[m % 2], 16)

            def step(i, j, first=False, last=False):
                if not (last and j + 2 >= BODY):
                    load_shift((j + 2) % BODY, BODY * i + j + 3)
                if j % OCT == 7 and not last:
                    sp.wait_ge(scores_ready, TB * (BODY * i + j + 1))
                    sp.wait_ge(pads_ready, 2)
                    load_stack(j // OCT, 2 * i + 2 + j // OCT)
                if j % HALF == 3 and not (first and j == 3):
                    m = j // HALF - 1
                    compact(i if m >= 0 else i - 1, m % QUADS)

            for n in range(len(qk_jobs)):
                store_parts(n)
            sp.wait_ge(gate_ready, T)
            sp.wait_ge(w_lo_ready, KC)
            sp.wait_ge(job_ready, JOB_V)
            sp.wait_ge(parts_stored[0], 64)
            load_stack(0, 0)
            sp.wait_ge(job_ready, JOBS)
            sp.wait_ge(parts_stored[1], 64)
            load_stack(1, 1)
            sp.wait_ge(parts_stored[2], 64 * (GROUPS - 2))
            sp.dma_start(ow_raw[:, :, :], ow.rearrange("(c p) n -> p c n", p=P)).then_inc(late_loaded, 16)
            sp.dma_start(ob_b[:, :], ob.partition_broadcast(P)).then_inc(late_loaded, 16)
            sp.dma_start(x_res[:, :, :], x_t).then_inc(late_loaded, 16)
            load_shift(0, 1)
            load_shift(1, 2)
            for j in range(BODY):
                step(0, j, first=True)
            with sp.Fori(1, TURNS - 1) as i:
                for j in range(BODY):
                    step(i, j)
            for j in range(BODY):
                step(TURNS - 1, j, last=True)
            compact(TURNS - 1, QUADS - 1)
            for t in range(T):
                sp.wait_ge(out_ready, t + 1)
                sp.dma_start(out_t[:, t, :], x_res[:, t, :]).then_inc(out_stored, 16)
            sp.wait_ge(out_stored, 16 * T)

        @block.tensor
        def _(pe):
            def begin(job):
                if job >= BANKS:
                    pe.wait_ge(job_evacuated, job - BANKS + 1)
                return bank[job % BANKS]

            def product(dst, stationary, moving):
                terms = [(0, 1), (1, 0), (0, 0)]
                n = 0
                for a, b in terms:
                    for c in range(KC):
                        mm = pe.matmul(dst, stationary(a, c), moving(b, c), start=(n == 0), stop=(n == 3 * KC - 1))
                        n += 1
                return mm

            xt, fwt, centt, w, oww = (xt_hi, xt_lo), (fwt_hi, fwt_lo), (centt_hi, centt_lo), (w_hi, w_lo), (ow_hi, ow_lo)
            ctxs = (ctx_hi, ctx_lo)

            pe.wait_ge(consts_ready, 1)
            for b in range(B):
                pe.wait_ge(xn_ready, TB * (b + 1))
                for c in range(KC):
                    dst = begin(JOB_XT + KC * b + c)
                    for t in range(TB):
                        mm = pe.transpose(dst[:, t * P:(t + 1) * P], xn[:, TB * b + t, c * P:(c + 1) * P], ident[:, :])
                    mm.then_inc(job_ready, 1)
            pe.wait_ge(fw_loaded, 16)
            for c in range(KC):
                dst = begin(JOB_WT + c)
                for o in range(N // P):
                    mm = pe.transpose(dst[:, o * P:(o + 1) * P], fw_raw[:, o, c * P:(c + 1) * P], ident[:, :])
                mm.then_inc(job_ready, 1)
            pe.wait_ge(cent_loaded, 32)
            dst = begin(JOB_CENT)
            for c in range(KC):
                pe.transpose(dst[:, c * CL:(c + 1) * CL], cent_raw[:, c * P:(c + 1) * P], ident[0:CL, 0:CL])
            pe.transpose(dst[:, KC * CL:KC * CL + 2 * KC], qkb_raw[:, :], ident[0:2 * KC, 0:2 * KC]).then_inc(job_ready, 1)
            pe.wait_ge(job_evacuated, JOB_CENT + 1)
            dst = begin(JOB_LOGITS)
            for t in range(T):
                mm = product(dst[:, t * CL:(t + 1) * CL], lambda a, c: xt[a][:, c, t * P:(t + 1) * P],
                             lambda b, c: centt[b][:, c, :])
            mm.then_inc(job_ready, 1)

            def dense(t):
                dst = begin(JOB_DENSE[t])
                product(dst, lambda a, c: xt[a][:, c, t * P:(t + 1) * P], lambda b, c: fwt[b][:, c, :]).then_inc(job_ready, 1)

            for t in range(3):
                dense(t)
            pe.wait_ge(hits_ready, 1)
            dst = begin(JOB_COUNT)
            for t in range(T):
                mm = pe.matmul(dst[0:CL, 0:P], hits[:, t, :], ones_bf[:, :], start=(t == 0), stop=(t == T - 1))
            mm.then_inc(job_ready, 1)
            dense(3)
            pe.wait_ge(onehot_ready, 1)
            pe.wait_ge(job_evacuated, JOB_COUNT + 1)
            pe.matmul(begin(JOB_ROWSEL), cl_sel[:, :], onehot[:, :], start=True, stop=True).then_inc(job_ready, 1)
            for t in range(4, T):
                dense(t)
            pe.wait_ge(w_lo_ready, KC)
            for n, (g, which) in enumerate(qk_jobs):
                b, o = g // OPB, g % OPB
                col = which * H + o * P
                dst = begin(JOB_QK + n)
                product(dst, lambda a, c: w[a][:, c, col:col + P],
                        lambda m, c: xt[m][:, c, b * S:(b + 1) * S]).then_inc(job_ready, 1)
            for t in range(T):
                dst = begin(JOB_V + t)
                product(dst, lambda a, c: xt[a][:, c, t * P:(t + 1) * P],
                        lambda m, c: w[m][:, c, 2 * H:3 * H]).then_inc(job_ready, 1)

            def max_scores(i, j, first=False):
                e, slot = j // OCT, j % OCT
                pe.wait_ge(stack_loaded[e], LOAD * i + LOAD)
                for u in range(2):
                    if first and j == 0:
                        pe.wait_ge(job_evacuated, JOB_V + 2 * u + 2)
                    else:
                        pe.wait_ge(maxes_ready, 2 * BODY * i + 2 * j + u - 1)
                    for v in range(2):
                        q = (2 * u + v) * P
                        mm = pe.matmul(max_tile[u][:, v, :], q_stack[e][0:ROWS_MAX, slot, q:q + P],
                                       k_stack[e][0:ROWS_MAX, slot, :], start=True, stop=True)
                    mm.then_inc(max_scores_ready, 1)

            def turn_shift(j, split):
                pe.wait_ge(shift_split, split)
                pe.wait_ge(shift_copied, split - 1)
                pe.matmul(turn_bank[0:2 * TB, 0:P], shift[:, j % OCT, :], ident[:, :], start=True, stop=True).then_inc(shift_turned, 1)

            def context(i, m, kt):
                if kt == 0:
                    quad = QUADS * i + m
                    pe.wait_ge(probs_ready, TB * HALF * (quad + 1))
                    pe.wait_ge(v_ready, quad + 1)
                    pe.wait_ge(ctx_evacuated, quad)
                for h in range(HALF):
                    a, b = (h, kt) if m % 2 == 0 else (kt, h)
                    mm = pe.matmul(ctx_bank[32 * h:32 * h + 32, :], v_ring[:, m % 2, kt, h, :], probs[:, a, b, :],
                                   start=(kt == 0), stop=(kt == TB - 1))
                mm.then_inc(probs_used, 1)

            def scores(i, j, first):
                e, slot = j // OCT, j % OCT
                pe.wait_ge(shift_loaded[slot], 32 * i + 16 * e + 16)
                for kt in range(TB):
                    if not (first and j == 0 and kt < 2):
                        pe.wait_ge(probs_ready, TB * BODY * i + TB * j + kt - 1)
                    pe.matmul(exp_tile[kt % 2], k_stack[e][0:ROWS_EXP, slot, kt * P:(kt + 1) * P],
                              q_stack[e][0:ROWS_EXP, slot, :], start=True, stop=True).then_inc(scores_ready, 1)

            def step(i, j, first=False, last=False):
                if not (last and j + 4 >= BODY):
                    max_scores(i if j + 4 < BODY else i + 1, (j + 4) % BODY)
                if j >= HALF:
                    context(i, j // HALF - 1, j % HALF)
                elif not first:
                    context(i - 1, QUADS - 1, j)
                if not (last and j + 2 >= BODY):
                    turn_shift((j + 2) % BODY, BODY * i + j + 3)
                scores(i, j, first)

            pe.wait_ge(pads_ready, 1)
            for j in range(4):
                max_scores(0, j, first=True)
            pe.wait_ge(job_evacuated, JOBS)
            turn_shift(0, 1)
            turn_shift(1, 2)
            for j in range(BODY):
                if j == 4:
                    pe.wait_ge(pads_ready, 2)
                step(0, j, first=True)
            with pe.Fori(1, TURNS - 1) as i:
                for j in range(BODY):
                    step(i, j)
            for j in range(BODY):
                step(TURNS - 1, j, last=True)
            for kt in range(TB):
                context(TURNS - 1, QUADS - 1, kt)

            pe.wait_ge(maxes_ready, 2 * OCT * GROUPS)
            pe.wait_ge(ow_ready, 1)
            for t in range(T):
                b, q = t // TB, (t % TB) * P
                if t % TB == 0:
                    pe.wait_ge(ctx_split, OPB * (b + 1))
                if t == 4:
                    pe.wait_ge(probs_ready, TB * OCT * GROUPS)
                if t == 6:
                    pe.wait_ge(shift_copied, OCT * GROUPS)
                if t == 7:
                    pe.wait_ge(ctx_evacuated, 2 * GROUPS)
                product(out_bank[t], lambda a, c: ctxs[a][:, OPB * b + c, q:q + P],
                        lambda m, c: oww[m][:, c, :]).then_inc(out_tile_ready, 1)

        @block.scalar
        def _(act):
            act.dma_start(cent_raw[:, :], cent).then_inc(cent_loaded, 16)
            act.dma_start(qkb_raw[:, :], qkvb[0:2 * H].rearrange("(c p) -> c p", p=P)).then_inc(cent_loaded, 16)
            act.dma_start(assign_b[:, :], assign.partition_broadcast(CL)).then_inc(small_loaded, 16)
            act.dma_start(fb_b[:, :], fb.partition_broadcast(P)).then_inc(small_loaded, 16)
            act.dma_start(row_bias[:, :], qkvb[2 * H:3 * H].partition_broadcast(P)).then_inc(small_loaded, 16)

            for n in range(SPLITS_A):
                act.wait_ge(job_ready, n + 1)
                if n < JOB_WT:
                    b, c = n // KC, n % KC
                    dst, src = xt_hi[:, c, b * S:(b + 1) * S], bank[n % BANKS]
                elif n < JOB_CENT:
                    dst, src = fwt_hi[:, n - JOB_WT, :], bank[n % BANKS]
                else:
                    dst, src = centt_hi[:, :, :].rearrange("p c k -> p (c k)"), bank[n % BANKS][:, 0:KC * CL]
                nc.scalar.copy(dst, src).then_inc(hi_ready, 1)
            act.wait_ge(job_evacuated, JOB_LOGITS + 1)
            nc.scalar.activation(expo[:, :, :], logit[:, :, :], ACT.Exp, scale=SHARP).then_inc(exp_ready, 1)
            for c in range(KC):
                act.wait_ge(w_loaded[c], 16)
                nc.scalar.copy(w_hi[:, c, :], w_stage[:, c % 2, :]).then_inc(w_hi_ready, 1)
            for t in range(T):
                act.wait_ge(masked_ready, t + 1)
                nc.scalar.activation(gate_exp[:, t, :], gate[:, t, :], ACT.Exp, scale=-1.0).then_inc(gate_exp_ready, 1)
            for n, (g, which) in enumerate(qk_jobs):
                act.wait_ge(job_ready, JOB_QK + n + 1)
                col = which * KC + g % OPB
                nc.scalar.activation((q_hi, k_hi)[which][:, g, :], bank[(JOB_QK + n) % BANKS], ACT.Identity,
                                     bias=qkb[:, col:col + 1]).then_inc(hi_ready, 1)

            def copy_shift(j, turned, loaded):
                act.wait_ge(shift_turned, turned)
                if loaded is not None:
                    act.wait_ge(shift_loaded[(j + HALF) % OCT], loaded)
                nc.scalar.copy(shift_row[:, j % HALF, :], turn_bank[0:2 * TB, 0:P]).then_inc(shift_copied, 1)

            def evacuate(i, m):
                quad = QUADS * i + m
                act.wait_ge(probs_used, TB * (quad + 1))
                if not (isinstance(i, int) and quad == 0):
                    act.wait_ge(compact_loaded[(m + 1) % 2], PACK * (2 * i + (m + 1) // 2))
                if m % 2 == 0 and not (isinstance(i, int) and quad == 0):
                    act.wait_ge(ctx_divided, 2 * i + m // 2)
                nc.scalar.copy(ctx_raw[:, :], ctx_bank).then_inc(ctx_evacuated, 1)

            def step(i, j, first=False, last=False):
                if j % HALF == 3 and not (first and j == 3):
                    m = j // HALF - 1
                    evacuate(i if m >= 0 else i - 1, m % QUADS)
                if not (last and j + 2 >= BODY):
                    back = (j - 2) // OCT
                    copy_shift((j + 2) % BODY, BODY * i + j + 3, None if first and j < 2 else 32 * i + 16 * back + 16)
                for kt in range(TB):
                    act.wait_ge(scores_ready, TB * (BODY * i + j) + kt + 1)
                    a, b = (j % HALF, kt) if j // HALF % 2 == 0 else (kt, j % HALF)
                    nc.scalar.activation(probs[:, a, b, :], exp_tile[kt % 2], ACT.Exp, scale=SCALE).then_inc(probs_ready, 1)

            copy_shift(0, 1, None)
            copy_shift(1, 2, None)
            for j in range(BODY):
                step(0, j, first=True)
            with act.Fori(1, TURNS - 1) as i:
                for j in range(BODY):
                    step(i, j)
            for j in range(BODY):
                step(TURNS - 1, j, last=True)
            evacuate(TURNS - 1, QUADS - 1)

        @block.vector
        def _(dve):
            steps = [0]

            def link(ins):
                steps[0] += 1
                ins.then_inc(dve_step, 1)
                dve.wait_ge(dve_step, steps[0])

            for b in range(B):
                tiles = range(TB * b, TB * (b + 1))
                for t in tiles:
                    dve.wait_ge(x_loaded[t], 16)
                    nc.vector.bn_stats(stats[:, t, :], xn[:, t, :]).then_inc(stats_done, 1)
                for t in tiles:
                    dve.wait_ge(stats_done, t + 1)
                    nc.vector.bn_aggr(mv[:, t, :], stats[:, t, :]).then_inc(aggr_done, 1)
                dve.wait_ge(aggr_done, TB * (b + 1))
                nc.vector.tensor_scalar_add(var_eps[:, TB * b:TB * (b + 1)], mv[:, TB * b:TB * (b + 1), 1], EPS).then_inc(var_ready, 1)
                dve.wait_ge(rstd_ready, b + 1)
                for t in tiles:
                    nc.vector.tensor_scalar(xn[:, t, :], xn[:, t, :], mv[:, t, 0:1], rstd[:, t:t + 1],
                                            ALU.subtract, ALU.mult).then_inc(xn_ready, 1)

            def evacuated(ins):
                ins.then_inc(job_evacuated, 1)

            for n in range(SPLITS_A):
                dve.wait_ge(hi_ready, n + 1)
                src = bank[n % BANKS]
                if n < JOB_WT:
                    b, c = n // KC, n % KC
                    hi, lo = xt_hi[:, c, b * S:(b + 1) * S], xt_lo[:, c, b * S:(b + 1) * S]
                elif n < JOB_CENT:
                    hi, lo = fwt_hi[:, n - JOB_WT, :], fwt_lo[:, n - JOB_WT, :]
                else:
                    link(nc.vector.tensor_copy(qkb[:, :], src[:, KC * CL:KC * CL + 2 * KC]))
                    src = src[:, 0:KC * CL]
                    hi, lo = (h[:, :, :].rearrange("p c k -> p (c k)") for h in (centt_hi, centt_lo))
                evacuated(nc.vector.tensor_tensor(lo, src, hi.bitcast(F32), ALU.subtract))

            dve.wait_ge(iota_ready, 1)
            link(nc.vector.tensor_copy(iota_f[:, :], iota_i[:, :]))
            dve.wait_ge(small_loaded, 48)
            nc.vector.tensor_scalar(onehot[:, :], assign_b[:, :], iota_f[:, 0:1], None, ALU.is_equal).then_inc(onehot_ready, 1)

            dve.wait_ge(job_ready, JOB_LOGITS + 1)
            lg = bank[JOB_LOGITS % BANKS].rearrange("p (t k) -> p t k", t=T)
            link(nc.vector.tensor_reduce(lmax[:, :], lg, AX.X, ALU.max))
            evacuated(nc.vector.tensor_tensor(logit[:, :, :], lg, lmax[:, :].unsqueeze(2).to_broadcast([P, T, CL]), ALU.subtract))

            def evacuate_dense(t):
                dve.wait_ge(job_ready, JOB_DENSE[t] + 1)
                evacuated(nc.vector.tensor_tensor(gate[:, t, :], bank[JOB_DENSE[t] % BANKS], fb_b[:, :], ALU.add))

            def mask(t):
                nc.vector.scalar_tensor_tensor(gate[:, t, :], gate[:, t, :], q_sel[:, t:t + 1], row_sel[:, :],
                                               ALU.mult, ALU.mult).then_inc(masked_ready, 1)

            evacuate_dense(0)
            dve.wait_ge(exp_ready, 1)
            link(nc.vector.tensor_reduce(thr[:, :], expo[:, :, :], AX.X, ALU.add))
            link(nc.vector.tensor_scalar(thr[:, :], thr[:, :], HIT, None, ALU.mult))
            nc.vector.tensor_tensor(hits[:, :, :], expo[:, :, :], thr[:, :].unsqueeze(2).to_broadcast([P, T, CL]),
                                    ALU.is_gt).then_inc(hits_ready, 1)
            dve.wait_ge(hits_ready, 1)
            link(nc.vector.tensor_reduce(q_sel[:, :], hits[:, :, :], AX.X, ALU.max))
            evacuate_dense(1)
            evacuate_dense(2)
            dve.wait_ge(job_ready, JOB_COUNT + 1)
            evacuated(nc.vector.tensor_scalar(cl_sel[:, :], bank[JOB_COUNT % BANKS][0:CL, 0:P], 0.5, None, ALU.is_gt))
            evacuate_dense(3)
            dve.wait_ge(job_ready, JOB_ROWSEL + 1)
            evacuated(nc.vector.tensor_copy(row_sel[:, :], bank[JOB_ROWSEL % BANKS]))
            dve.wait_ge(job_evacuated, JOB_ROWSEL + 1)
            for t in range(4):
                mask(t)
            for t in range(4, T):
                evacuate_dense(t)
                dve.wait_ge(job_evacuated, JOB_DENSE[t] + 1)
                mask(t)

            for n, (g, which) in enumerate(qk_jobs):
                dve.wait_ge(hi_ready, SPLITS_A + n + 1)
                col = which * KC + g % OPB
                evacuated(nc.vector.scalar_tensor_tensor(
                    (q_lo, k_lo)[which][:, g, :], bank[(JOB_QK + n) % BANKS], qkb[:, col:col + 1],
                    (q_hi, k_hi)[which][:, g, :].bitcast(F32), ALU.add, ALU.subtract))
                if n % 2:
                    dve.wait_ge(gate_den_ready, n // 2 + 1)
                    nc.vector.reciprocal(gate_exp[:, n // 2, :], gate_exp[:, n // 2, :]).then_inc(gate_inverted, 1)
            dve.wait_ge(gate_ready, T)
            for t in range(T):
                b, kt = t // TB, t % TB
                dve.wait_ge(job_ready, JOB_V + t + 1)
                evacuated(nc.vector.tensor_tensor(
                    v_all[:, b * OPB:(b + 1) * OPB, kt, :], bank[(JOB_V + t) % BANKS].rearrange("p (o c) -> p o c", o=OPB),
                    row_bias[:, :].rearrange("p (o c) -> p o c", o=OPB), ALU.add))

            def invert(g):
                dve.wait_ge(compact_loaded[0], PACK * (g + 1))
                dve.wait_ge(compact_loaded[1], PACK * (g + 1))
                nc.vector.reciprocal(den_c[:, :], den_c[:, :]).then_inc(den_inverted, 1)

            def maxima(i, first=False):
                for j in range(BODY):
                    if not first and j % OCT == 1:
                        invert(2 * i - 2 + j // OCT)
                    if not (first and j < OCT):
                        dve.wait_ge(shift_split, BODY * i + j + 1 - OCT)
                    for u in range(2):
                        dve.wait_ge(max_scores_ready, 2 * (BODY * i + j) + u + 1)
                        nc.vector.tensor_reduce(neg_max[:, j % OCT, 2 * u:2 * u + 2], max_tile[u][:, :, :], AX.X, ALU.max,
                                                negate=True).then_inc(maxes_ready, 1)

            maxima(0, first=True)
            with dve.Fori(1, TURNS) as i:
                maxima(i)
            invert(GROUPS - 2)

            dve.wait_ge(late_loaded, 48)
            dve.wait_ge(v_ready, QUADS * TURNS)
            link(nc.vector.tensor_copy(ow_hi[:, :, :], ow_raw[:, :, :]))
            nc.vector.tensor_tensor(ow_lo[:, :, :], ow_raw[:, :, :], ow_hi[:, :, :].bitcast(F32), ALU.subtract).then_inc(ow_ready, 1)
            for t in range(T):
                link(nc.vector.tensor_tensor(ob_gate[:, :], ob_b[:, :], gate[:, t, :], ALU.mult))
                link(nc.vector.tensor_tensor(x_res[:, t, :], x_res[:, t, :], ob_gate[:, :], ALU.add))
            invert(GROUPS - 1)
            for t in range(T):
                dve.wait_ge(out_tile_ready, t + 1)
                nc.vector.tensor_tensor(gate[:, t, :], out_bank[t], gate[:, t, :], ALU.mult).then_inc(gated_ready, 1)
                dve.wait_ge(gated_ready, t + 1)
                nc.vector.tensor_tensor(x_res[:, t, :], x_res[:, t, :], gate[:, t, :], ALU.add).then_inc(out_ready, 1)

        @block.gpsimd
        def _(pool):
            steps = [0]

            def link(ins):
                steps[0] += 1
                ins.then_inc(pool_step, 1)
                pool.wait_ge(pool_step, steps[0])

            nc.gpsimd.memset(neg_half[:, :], -0.5)
            nc.gpsimd.memset(zeros[:, :], 0.0)
            link(nc.gpsimd.memset(ident[:, :], 0.0))
            nc.gpsimd.affine_select(out=ident[:, :], in_=ident[:, :], compare_op=ALU.not_equal, fill=1.0, base=0,
                                    pattern=[[-1, P]], channel_multiplier=1).then_inc(consts_ready, 1)
            nc.gpsimd.iota(iota_i[:, :], [[0, 1]], base=0, channel_multiplier=1).then_inc(iota_ready, 1)
            link(nc.gpsimd.memset(ones_bf[:, :], 1.0))
            for b in range(B):
                pool.wait_ge(var_ready, b + 1)
                r = slice(TB * b, TB * (b + 1))
                nc.gpsimd.tensor_tensor(rstd[:, r], var_eps[:, r], neg_half[:, r], ALU.pow).then_inc(rstd_ready, 1)
            for c in range(KC):
                pool.wait_ge(w_hi_ready, c + 1)
                nc.gpsimd.tensor_tensor(w_lo[:, c, :], w_stage[:, c % 2, :], w_hi[:, c, :].bitcast(F32),
                                        ALU.subtract).then_inc(w_lo_ready, 1)
            for t in range(T):
                pool.wait_ge(gate_exp_ready, t + 1)
                nc.gpsimd.tensor_scalar(gate_exp[:, t, :], gate_exp[:, t, :], 1.0, None, ALU.add).then_inc(gate_den_ready, 1)
            for t in range(T):
                pool.wait_ge(gate_inverted, t + 1)
                nc.gpsimd.tensor_tensor(gate[:, t, :], gate[:, t, :], gate_exp[:, t, :], ALU.mult).then_inc(gate_ready, 1)
            pool.wait_ge(gate_ready, T)
            pool.wait_ge(w_lo_ready, KC)

            def pads(e):
                link(nc.gpsimd.memset(q_stack[e][64:ROWS_MAX, :, :].bitcast(F32), 0.0))
                link(nc.gpsimd.memset(k_stack[e][64:ROWS_MAX, :, :].bitcast(F32), 0.0))
                nc.gpsimd.memset(k_stack[e][ROW_SHIFT:ROWS_EXP, :, :].bitcast(F32), 1.0).then_inc(pads_ready, 1)
                pool.wait_ge(pads_ready, e + 1)

            pool.wait_ge(job_ready, JOB_V)
            pads(0)
            pool.wait_ge(job_ready, JOBS)
            link(nc.gpsimd.memset(v_ring[:, :, :, :, HD:2 * HD], 1.0))
            def split_shift(i, j, first=False):
                head, slot = BODY * i + j, j % OCT
                pool.wait_ge(maxes_ready, 2 * head + 2)
                if not (first and j < OCT):
                    pool.wait_ge(shift_turned, head + 1 - OCT)
                nc.gpsimd.tensor_tensor(shift[:, slot, 0:TB].bitcast(F32R), neg_max[:, slot, :], zeros[:, :],
                                        ALU.add).then_inc(shift_hi_ready, 1)
                pool.wait_ge(shift_hi_ready, head + 1)
                nc.gpsimd.tensor_tensor(shift[:, slot, TB:2 * TB], neg_max[:, slot, :], shift[:, slot, 0:TB],
                                        ALU.subtract).then_inc(shift_split, 1)

            def group(buffer, g):
                return buffer[:, bass.ds(g, 1), :].rearrange("p a s -> p (a s)")

            def fill_v(i, m):
                quad, e = QUADS * i + m, m % 2
                if not (isinstance(i, int) and quad < 2):
                    pool.wait_ge(probs_used, TB * (quad - 1))
                cols = slice(HALF * HD * e, HALF * HD * (e + 1))
                nc.gpsimd.tensor_copy(
                    v_ring[:, e, :, :, 0:HD],
                    v_all[:, bass.ds(2 * i + m // 2, 1), :, cols].rearrange("p a t (h d) -> p (a t) h d", d=HD)).then_inc(v_ready, 1)

            def divide(g):
                pool.wait_ge(den_inverted, g + 1)
                nc.gpsimd.tensor_tensor(ctx_n[:, :], ctx_c[:, :], den_c[:, :], ALU.mult).then_inc(ctx_divided, 1)

            def context_hi(g):
                pool.wait_ge(ctx_divided, g + 1)
                nc.gpsimd.tensor_copy(group(ctx_hi, g), ctx_n[:, :]).then_inc(ctx_hi_ready, 1)

            def context_lo(g):
                pool.wait_ge(ctx_hi_ready, g + 1)
                nc.gpsimd.tensor_tensor(group(ctx_lo, g), ctx_n[:, :], group(ctx_hi, g).bitcast(F32),
                                        ALU.subtract).then_inc(ctx_split, 1)
                pool.wait_ge(ctx_split, g + 1)

            def steps_of(i, first=False):
                for j in range(BODY):
                    split_shift(i, j, first)
                    if j % HALF == 0 and not (first and j == 0):
                        m = j // HALF - 1
                        fill_v(i if m >= 0 else i - 1, m % QUADS)
                    if not first:
                        g = 2 * i - 2 + j // OCT
                        if j % OCT == 2:
                            divide(g)
                        if j % OCT == 3:
                            context_hi(g)
                        if j % OCT == 5:
                            context_lo(g)
                    if first and j == 2:
                        pool.wait_ge(shift_split, j + 1)
                        pads(1)

            steps_of(0, first=True)
            with pool.Fori(1, TURNS) as i:
                steps_of(i)
            fill_v(TURNS - 1, QUADS - 1)
            for g in range(GROUPS - 2, GROUPS):
                divide(g)
                context_hi(g)
                context_lo(g)


_INS = ["L0_attn_x", "L0_attn_attn_qkvw", "L0_attn_attn_qkvb", "L0_attn_attn_ow", "L0_attn_attn_ob",
        "L0_ffn_weight", "L0_ffn_bias", "L0_ffn_centroids", "L0_ffn_assignments"]


def kernel(**inputs):
    import numpy as _np
    import concourse.bacc as _bacc
    from concourse import mybir as _mybir
    from concourse.bass_utils import run_bass_kernel_spmd as _run

    nc = _bacc.Bacc("TRN2", target_bir_lowering=False, num_devices=1)
    arrays, args = {}, []
    for name in _INS:
        a = _np.ascontiguousarray(inputs[name])
        arrays[f"in_{name}"] = a
        args.append(nc.dram_tensor(f"in_{name}", a.shape, _mybir.dt.from_np(a.dtype), kind="ExternalInput").ap())
    shape = arrays["in_L0_attn_x"].shape
    out = nc.dram_tensor("out_x", shape, _mybir.dt.float32, kind="ExternalOutput").ap()
    build(nc, *args, out)
    r = _run(nc, [arrays], core_ids=[0])
    return r.results[0]["out_x"]
```

```python
from contextlib import ExitStack

import concourse.bass as bass
from concourse import mybir

F32 = mybir.dt.float32
F32R = mybir.dt.float32r
BF16 = mybir.dt.bfloat16
I32 = mybir.dt.int32
ALU = mybir.AluOpType
ACT = mybir.ActivationFunctionType
AX = mybir.AxisListType

P = 128
BANK = 512
BANKS = 8


def build(nc, x, qkvw, qkvb, ow, ob, fw, fb, cent, assign, out):
    B, S, H = x.shape
    N = fw.shape[0]
    CL = cent.shape[0]
    HD = 16
    HEADS = H // HD
    T = B * S // P
    TB = S // P
    KC = H // P
    OCT = P // HD
    GROUPS = B * HEADS // OCT
    OPB = GROUPS // B
    HALF = OCT // 2
    EPS = 1e-5
    SHARP = 10.0
    HIT = 0.01
    SCALE = HD ** -0.5
    ROWS_MAX, ROW_SHIFT, ROWS_EXP = 96, 96, 98
    BODY = 2 * OCT
    TURNS = B * HEADS // BODY
    QUADS = BODY // HALF
    PAIRS = BODY // 2
    OCT_PAIRS = OCT // 2
    AHEAD, CATCH_UP = 5, 5
    PIECES = 4
    LOAD = PIECES * 16
    PACK = HALF * 16
    assert S == BANK and N == BANK and H == 4 * P and T == 8 and KC == TB == 4 and CL == 64

    def turned_beside(i, j, first, last):
        if first and j <= CATCH_UP + 1:
            pair = None if j % 2 else j // 2 + 1
        else:
            pair = (j + 3) // 2 if j % 2 else None
        if pair is None or (last and pair >= PAIRS):
            return None
        return (i, pair) if pair < PAIRS else (i + 1, pair - PAIRS)

    x_t = x.rearrange("b (t p) h -> p (b t) h", p=P)
    out_t = out.rearrange("b (t p) h -> p (b t) h", p=P)
    w_c = qkvw.rearrange("(c p) n -> p c n", p=P)

    JOB_XT, JOB_WT, JOB_CENT = [0, 1, 6, 7, 13, 14, 15, 16], [2, 3, 4, 5], 8
    JOB_LOGITS_T, JOB_LOGITS = (11, 18), 20
    JOB_DENSE = [9, 10, 12, 17, 19, 21, 22, 24]
    JOB_COUNT, JOB_ROWSEL, JOB_QK, JOB_V = 23, 25, 26, 42
    JOBS = 50
    BANK_OF = [n % BANKS if n < JOB_V else 4 + (n - JOB_V + 1) % 3 for n in range(JOBS)]
    SPLITS_A = sorted([*JOB_XT, *JOB_WT, JOB_CENT])
    qk_jobs = [(g, which) for g in range(GROUPS) for which in range(2)]

    parts_dram = nc.dram_tensor("qk_parts", [2, GROUPS, 2, HD, OCT, S], F32, kind="Internal").ap()
    inv_dram = nc.dram_tensor("inverses", [2, HALF, 2 * S], F32, kind="Internal").ap()

    with ExitStack() as ctx:
        def sem(name):
            return ctx.enter_context(nc.semaphore(name))

        def sems(name, n):
            return [sem(f"{name}{i}") for i in range(n)]

        start = (nc.sbuf_base + 63) // 64 * 64
        KB = 1024

        def at(name, offset, shape, dt):
            return nc.alloc_sbuf_tensor_at(name, shape, dt, offset=start + offset)

        QK, V, G, X, STAGE, WHI, WLO, XT, ROW, SMALL = (n * KB for n in (0, 64, 80, 96, 112, 124, 148, 172, 204, 206))
        q_hi = at("q_hi", QK, [P, GROUPS, S], F32R)
        q_lo = at("q_lo", QK + 16 * KB, [P, GROUPS, S], F32R)
        k_hi = at("k_hi", QK + 32 * KB, [P, GROUPS, S], F32R)
        k_lo = at("k_lo", QK + 48 * KB, [P, GROUPS, S], F32R)
        v_all = at("v_all", V, [P, GROUPS, TB, P], F32)
        gate = at("gate", G, [P, T, N], F32)
        xn = at("xn", X, [P, T, H], F32)
        gate_exp = at("gate_exp", X, [P, T, N], F32)
        w_stage = at("w_stage", STAGE, [P, 2, 3 * H], F32)
        w_hi = at("w_hi", WHI, [P, KC, 3 * H], F32R)
        w_lo = at("w_lo", WLO, [P, KC, 3 * H], F32R)
        xt_hi = at("xt_hi", XT, [P, KC, T * P], F32R)
        xt_lo = at("xt_lo", XT + 16 * KB, [P, KC, T * P], F32R)
        fw_raw = at("fw_raw", QK, [P, KC, H], F32)
        fwt_hi = at("fwt_hi", QK + 8 * KB, [P, KC, N], F32R)
        fwt_lo = at("fwt_lo", QK + 16 * KB, [P, KC, N], F32R)
        cent_raw = at("cent_raw", QK + 24 * KB, [CL, H], F32)
        centt_hi = at("centt_hi", QK + 26 * KB, [P, KC, CL], F32R)
        centt_lo = at("centt_lo", QK + 27 * KB, [P, KC, CL], F32R)
        qkb_raw = at("qkb_raw", QK + 28 * KB, [2 * KC, P], F32)
        logit = at("logit", V, [P, T, CL], F32)
        expo = at("expo", V + 2 * KB, [P, T, CL], F32)
        hits = at("hits", V + 4 * KB, [P, T, CL], BF16)
        onehot = at("onehot", V + 5 * KB, [CL, N], BF16)
        assign_b = at("assign_b", V + 6 * KB, [CL, N], I32)
        row_sel = at("row_sel", V + 8 * KB, [P, N], F32)
        fb_b = at("fb_b", V + 10 * KB, [P, N], F32)
        logit_t = at("logit_t", V + 12 * KB, [CL, T, P], F32)
        ident = at("ident", SMALL, [P, P], F32)
        row_bias = at("row_bias", ROW, [P, N], F32)
        small = SMALL + 512
        ones_bf = at("ones_bf", small, [P, P], BF16)
        cl_sel = at("cl_sel", small + 256, [CL, P], BF16)
        stats = at("stats", small + 512, [P, T, 6], F32)
        mv = at("mv", small + 704, [P, T, 2], F32)
        var_eps = at("var_eps", small + 768, [P, T], F32)
        rstd = at("rstd", small + 800, [P, T], F32)
        neg_half = at("neg_half", small + 832, [P, T], F32)
        qkb = at("qkb", small + 864, [P, 2 * KC], F32)
        lmax = at("lmax", small + 896, [P, T], F32)
        thr = at("thr", small + 928, [P, T], F32)
        q_sel = at("q_sel", small + 960, [P, T], F32)
        zeros = at("zeros", small + 1056, [P, 2 * TB], F32)
        iota_i = at("iota_i", small + 992, [CL, 1], I32)
        iota_f = at("iota_f", small + 1024, [CL, 1], F32)
        shift = at("shift", small, [P, OCT_PAIRS, 2, 2 * TB], F32)
        neg_max = at("neg_max", small + 512, [P, OCT, TB], F32)
        den = at("den", small + 704, [P, 2, OCT * S // P], F32)
        BUF = STAGE + 16 * KB
        q_stack = [at("q_stack0", X, [P, OCT, S], F32R), at("q_stack1", BUF, [P, OCT, S], F32R)]
        k_stack = [at("k_stack0", STAGE, [P, OCT, S], F32R), at("k_stack1", BUF + 16 * KB, [P, OCT, S], F32R)]
        probs = at("probs", BUF + 32 * KB, [P, HALF, HALF, S], F32)
        v_ring = at("v_ring", BUF + 64 * KB, [P, 2, TB, HALF, 2 * HD], F32)
        ctx_c = at("ctx_c", BUF + 68 * KB, [P, 2, S], F32)
        inv_b = at("inv_b", BUF + 72 * KB, [P, 2, S], F32)
        x_res = at("x_res", QK + 32 * KB, [P, T, H], F32)
        ow_raw = at("ow_raw", QK + 48 * KB, [P, KC, H], F32)
        ob_b = at("ob_b", QK + 56 * KB, [P, H], F32)
        shift_row = at("shift_row", QK + 58 * KB, [4 * TB, 2, P], F32)
        ctx_raw = at("ctx_raw", QK + 60 * KB, [P, 2, S], F32)
        ow_hi = at("ow_hi", V, [P, KC, H], F32R)
        ow_lo = at("ow_lo", QK + 48 * KB, [P, KC, H], F32R)
        ctx_hi, ctx_lo = q_hi, q_lo
        ob_gate = at("ob_gate", ROW, [P, H], F32)

        pairs = [ctx.enter_context(nc.psum_tensor(f"banks{2 * i}", [P, 2, BANK], F32)) for i in range(4)]
        bank = [pairs[i // 2][:, i % 2, :] for i in range(BANKS)]
        max_tile = [pairs[0], pairs[1]]
        exp_tile = [bank[4], bank[5]]
        ctx_bank, turn_bank = bank[6], bank[7]

        x_loaded = sems("x_loaded", T)
        fw_loaded = sems("fw_loaded", KC)
        cent_loaded, small_loaded = sem("cent_loaded"), sem("small_loaded")
        w_loaded = sems("w_loaded", KC)
        consts_ready, iota_ready = sem("consts_ready"), sem("iota_ready")
        stats_done, aggr_done, var_ready, rstd_ready, xn_ready = (
            sem("stats_done"), sem("aggr_done"), sem("var_ready"), sem("rstd_ready"), sem("xn_ready"))
        onehot_ready = sem("onehot_ready")
        job_ready, hi_ready, job_evacuated = sem("job_ready"), sem("hi_ready"), sem("job_evacuated")
        dve_step, pool_step = sem("dve_step"), sem("pool_step")
        exp_ready, hits_ready = sem("exp_ready"), sem("hits_ready")
        w_hi_ready, w_lo_ready = sem("w_hi_ready"), sem("w_lo_ready")
        masked_ready, gate_exp_ready, gate_ready = sem("masked_ready"), sem("gate_exp_ready"), sem("gate_ready")
        pads_ready, pads_copied, ones_ready = sem("pads_ready"), sem("pads_copied"), sem("ones_ready")
        parts_stored = sems("parts_stored", 3)
        stack_loaded = sems("stack_loaded", 2)
        shift_loaded = sems("shift_loaded", OCT_PAIRS)
        max_scores_ready, maxes_ready, shift_split = sem("max_scores_ready"), sem("maxes_ready"), sem("shift_split")
        shift_turned, shift_copied = sem("shift_turned"), sem("shift_copied")
        scores_ready, probs_ready, probs_used = sem("scores_ready"), sem("probs_ready"), sem("probs_used")
        v_ready, ctx_evacuated = sem("v_ready"), sem("ctx_evacuated")
        ctx_packed, den_loaded = sems("ctx_packed", 2), sems("den_loaded", 2)
        den_inverted, inv_stored, inv_loaded = sem("den_inverted"), sem("inv_stored"), sem("inv_loaded")
        gate_den_ready, gate_inverted = sem("gate_den_ready"), sem("gate_inverted")
        ctx_divided, ctx_hi_ready, ctx_split = sem("ctx_divided"), sem("ctx_hi_ready"), sem("ctx_split")
        shift_hi_ready = sem("shift_hi_ready")
        late_loaded = sem("late_loaded")
        ow_hi_ready, ow_ready, rest_ready, bias_gated = sem("ow_hi_ready"), sem("ow_ready"), sem("rest_ready"), sem("bias_gated")
        out_tile_ready, gated_ready, out_ready, out_stored = (
            sem("out_tile_ready"), sem("gated_ready"), sem("out_ready"), sem("out_stored"))

        block = ctx.enter_context(nc.Block())

        @block.sync
        def _(sp):
            for b in range(B):
                for t in range(TB * b, TB * (b + 1)):
                    sp.dma_start(xn[:, t, :], x_t[:, t, :]).then_inc(x_loaded[t], 16)
                if b == 0:
                    for c in range(KC):
                        sp.dma_start(fw_raw[:, :, c * P:(c + 1) * P],
                                     fw.rearrange("(o p) h -> p o h", p=P)[:, :, c * P:(c + 1) * P]).then_inc(fw_loaded[c], 16)
            for c in range(KC):
                if c >= 2:
                    sp.wait_ge(w_lo_ready, c - 1)
                sp.dma_start(w_stage[:, c % 2, :], w_c[:, c, :]).then_inc(w_loaded[c], 16)

            def store_parts(n):
                g, which = qk_jobs[n]
                sp.wait_ge(job_evacuated, JOB_QK + n + 1)
                for part, src in enumerate(((q_hi, q_lo), (k_hi, k_lo))[which]):
                    sp.dma_start(parts_dram[which, g, part].rearrange("d j s -> j d s"),
                                 src[:, g, :].bitcast(F32)).then_inc(parts_stored[min(g, 2)], 16)

            def load_stack(e, g, piece):
                q, k = (parts_dram[which, bass.ds(g, 1)].rearrange("a x d j s -> (a x d) (j s)") for which in range(2))
                half = slice(2 * HD * (piece % 2), 2 * HD * (piece % 2 + 1))
                if piece < 2:
                    stack, src = q_stack, q[0:2 * HD]
                else:
                    rows = k[HD * (piece % 2):HD * (piece % 2 + 1)]
                    stack, src = k_stack, bass.AP(tensor=rows.tensor, offset=rows.offset, ap=[[0, 2], *rows.ap])
                sp.dma_start(stack[e][half, :, :].bitcast(F32), src).then_inc(stack_loaded[e], 16)

            def load_shift(i, pair):
                sp.wait_ge(shift_copied, PAIRS * i + pair + 1)
                slot = 2 * (pair % OCT_PAIRS)
                sp.dma_start(
                    q_stack[pair // OCT_PAIRS][ROW_SHIFT:ROW_SHIFT + 2, slot:slot + 2, :].rearrange("r h (t q) -> r (h t) q", t=TB).bitcast(F32),
                    shift_row[:, pair % 2, :]).then_inc(shift_loaded[pair % OCT_PAIRS], 16)

            def pack_den(i, r):
                sp.wait_ge(ctx_evacuated, QUADS * i + 2 * r + 2)
                sp.dma_start(den[:, r, :], ctx_raw[HD:P:32, :, :]).then_inc(den_loaded[r], 16)

            def pack_context(i, r, heads):
                if r == 0 and not (isinstance(i, int) and i == 0):
                    sp.wait_ge(ctx_divided, 2 * i)
                for h in heads:
                    row = HALF * HD * r + HD * h
                    sp.dma_start(ctx_c[row:row + HD, :, :], ctx_raw[32 * h:32 * h + HD, :, :]).then_inc(ctx_packed[r], 16)

            def store_inverses(i):
                sp.wait_ge(den_inverted, i + 1)
                sp.dma_start(inv_dram.rearrange("r h (p n) -> (h p) r n", n=OCT * S // P),
                             den[:, :, :]).then_inc(inv_stored, 16)

            def load_inverses(i):
                sp.wait_ge(inv_stored, 16 * i + 16)
                for r in range(2):
                    rows = inv_dram[r]
                    each = bass.AP(tensor=rows.tensor, offset=rows.offset, ap=[rows.ap[0], [0, HD], rows.ap[1]])
                    sp.dma_start(inv_b[HALF * HD * r:HALF * HD * (r + 1), :, :], each).then_inc(inv_loaded, 16)

            def step(i, j, first=False, last=False):
                beside = turned_beside(i, j, first, last)
                if beside:
                    load_shift(*beside)
                if j % OCT == 7 and not last:
                    sp.wait_ge(scores_ready, TB * (BODY * i + j + 1))
                    sp.wait_ge(pads_copied, 16)
                    for piece in range(PIECES // 2):
                        load_stack(j // OCT, 2 * i + 2 + j // OCT, piece)
                for piece in range(PIECES // 2, PIECES):
                    if j == 0 and not first:
                        load_stack(1, 2 * i + 1, piece)
                    if j == OCT and not last:
                        load_stack(0, 2 * i + 2, piece)
                packed, r = (i, 0) if j >= OCT else (i - 1, 1)
                if j >= OCT or not first:
                    if j % OCT == 2:
                        pack_den(packed, r)
                        pack_context(packed, r, (0,))
                    if j % OCT == 3:
                        pack_context(packed, r, (1, 2, 3))
                if not first and j == 5:
                    store_inverses(i - 1)
                if not first and j == 6:
                    load_inverses(i - 1)

            for n in range(len(qk_jobs) - 1):
                store_parts(n)
            sp.wait_ge(gate_ready, T)
            sp.wait_ge(w_lo_ready, KC)
            sp.wait_ge(job_ready, JOB_V)
            sp.wait_ge(parts_stored[0], 64)
            for piece in range(PIECES):
                load_stack(0, 0, piece)
            store_parts(len(qk_jobs) - 1)
            sp.wait_ge(parts_stored[1], 64)
            sp.wait_ge(parts_stored[2], 64 * (GROUPS - 2))
            load_shift(0, 0)
            sp.wait_ge(job_ready, JOBS)
            sp.wait_ge(pads_ready, 2)
            for piece in range(PIECES // 2):
                load_stack(1, 1, piece)
            for j in range(BODY):
                step(0, j, first=True)
                if j == 0:
                    for piece in range(PIECES // 2, PIECES):
                        load_stack(1, 1, piece)
                if j == 1:
                    rows = slice(4 * HD, ROWS_EXP)
                    sp.dma_start(k_stack[1][rows, :, :].bitcast(F32), k_stack[0][rows, :, :].bitcast(F32)).then_inc(pads_copied, 16)
                if 4 <= j < 4 + OPB // 2:
                    ow_rows = ow.rearrange("(a r c p) n -> a r p c n", a=OPB // 2, r=2, c=2)
                    a = j - 4
                    for r in range(2):
                        sp.dma_start(ow_raw[HALF * HD * r:HALF * HD * (r + 1), 2 * a:2 * a + 2, :],
                                     ow_rows[a, r]).then_inc(late_loaded, 16)
                if j == 6:
                    sp.dma_start(ob_b[:, :], ob.partition_broadcast(P)).then_inc(late_loaded, 16)
                if j >= OCT:
                    t = j - OCT
                    sp.dma_start(x_res[:, t, :], x_t[:, t, :]).then_inc(late_loaded, 16)
            with sp.Fori(1, TURNS - 1) as i:
                for j in range(BODY):
                    step(i, j)
            for j in range(BODY):
                step(TURNS - 1, j, last=True)
            pack_den(TURNS - 1, 1)
            pack_context(TURNS - 1, 1, range(HALF))
            store_inverses(TURNS - 1)
            load_inverses(TURNS - 1)
            for t in range(T):
                sp.wait_ge(out_ready, t + 1)
                sp.dma_start(out_t[:, t, :], x_res[:, t, :]).then_inc(out_stored, 16)
            sp.wait_ge(out_stored, 16 * T)

        @block.tensor
        def _(pe):
            def begin(job):
                before = [n for n in range(job) if BANK_OF[n] == BANK_OF[job]]
                if before:
                    pe.wait_ge(job_evacuated, before[-1] + 1)
                return bank[BANK_OF[job]]

            def product(dst, stationary, moving, part=range(3 * KC)):
                for n in part:
                    (a, b), c = ((0, 1), (1, 0), (0, 0))[n // KC], n % KC
                    mm = pe.matmul(dst, stationary(a, c), moving(b, c), start=(n == 0), stop=(n == 3 * KC - 1))
                return mm

            xt, fwt, centt, w, oww = (xt_hi, xt_lo), (fwt_hi, fwt_lo), (centt_hi, centt_lo), (w_hi, w_lo), (ow_hi, ow_lo)
            ctxs = (ctx_hi, ctx_lo)

            def x_transposed(t):
                pe.wait_ge(xn_ready, t + 1)
                dst = begin(JOB_XT[t])
                for c in range(KC):
                    mm = pe.transpose(dst[:, c * P:(c + 1) * P], xn[:, t, c * P:(c + 1) * P], ident[:, :])
                mm.then_inc(job_ready, 1)

            def logits_transposed(b):
                pe.wait_ge(job_evacuated, max(JOB_CENT, JOB_XT[TB * b + TB - 1]) + 1)
                dst = begin(JOB_LOGITS_T[b])
                product(dst[0:CL, :], lambda a, c: centt[a][:, c, :],
                        lambda m, c: xt[m][:, c, b * S:(b + 1) * S]).then_inc(job_ready, 1)

            def dense(t):
                pe.wait_ge(job_evacuated, JOB_XT[t] + 1)
                dst = begin(JOB_DENSE[t])
                product(dst, lambda a, c: xt[a][:, c, t * P:(t + 1) * P], lambda b, c: fwt[b][:, c, :]).then_inc(job_ready, 1)

            pe.wait_ge(consts_ready, 1)
            x_transposed(0)
            x_transposed(1)
            for c in range(KC):
                pe.wait_ge(fw_loaded[c], 16)
                dst = begin(JOB_WT[c])
                for o in range(N // P):
                    mm = pe.transpose(dst[:, o * P:(o + 1) * P], fw_raw[:, o, c * P:(c + 1) * P], ident[:, :])
                mm.then_inc(job_ready, 1)
            x_transposed(2)
            x_transposed(3)
            pe.wait_ge(cent_loaded, 32)
            dst = begin(JOB_CENT)
            for c in range(KC):
                pe.transpose(dst[:, c * CL:(c + 1) * CL], cent_raw[:, c * P:(c + 1) * P], ident[0:CL, 0:CL])
            pe.transpose(dst[:, KC * CL:KC * CL + 2 * KC], qkb_raw[:, :], ident[0:2 * KC, 0:2 * KC]).then_inc(job_ready, 1)
            pe.wait_ge(job_evacuated, JOB_WT[-1] + 1)
            dense(0)
            dense(1)
            logits_transposed(0)
            dense(2)
            for t in range(TB, T):
                x_transposed(t)
            dense(TB - 1)
            logits_transposed(1)
            dense(4)
            dst = begin(JOB_LOGITS)
            pe.wait_ge(job_evacuated, JOB_LOGITS_T[1] + 1)
            for t in range(T):
                mm = pe.transpose(dst[:, t * CL:(t + 1) * CL], logit_t[:, t, :], ident[0:CL, 0:CL])
            mm.then_inc(job_ready, 1)
            dense(5)
            dense(6)
            pe.wait_ge(hits_ready, 1)
            dst = begin(JOB_COUNT)
            for t in range(T):
                mm = pe.matmul(dst[0:CL, 0:P], hits[:, t, :], ones_bf[:, :], start=(t == 0), stop=(t == T - 1))
            mm.then_inc(job_ready, 1)
            dense(7)
            pe.wait_ge(onehot_ready, 1)
            pe.wait_ge(job_evacuated, JOB_COUNT + 1)
            pe.matmul(begin(JOB_ROWSEL), cl_sel[:, :], onehot[:, :], start=True, stop=True).then_inc(job_ready, 1)
            pe.wait_ge(w_lo_ready, KC)
            for n, (g, which) in enumerate(qk_jobs):
                b, o = g // OPB, g % OPB
                col = which * H + o * P
                dst = begin(JOB_QK + n)
                product(dst, lambda a, c: w[a][:, c, col:col + P],
                        lambda m, c: xt[m][:, c, b * S:(b + 1) * S]).then_inc(job_ready, 1)

            def max_scores(i, j, q, first=False):
                e, slot = j // OCT, j % OCT
                if q == 0:
                    pe.wait_ge(stack_loaded[e], LOAD * i + LOAD)
                if q % 2 == 0:
                    if first and j == 0:
                        pe.wait_ge(job_evacuated, JOB_V)
                    else:
                        pe.wait_ge(maxes_ready, 2 * BODY * i + 2 * j + q // 2 - 1)
                mm = pe.matmul(max_tile[q // 2][:, q % 2, :], q_stack[e][0:ROWS_MAX, slot, q * P:(q + 1) * P],
                               k_stack[e][0:ROWS_MAX, slot, :], start=True, stop=True)
                if q % 2:
                    mm.then_inc(max_scores_ready, 1)

            def turn_shift(i, pair):
                pe.wait_ge(shift_split, PAIRS * i + pair + 1)
                if not (isinstance(i, int) and i == pair == 0):
                    pe.wait_ge(shift_copied, PAIRS * i + pair)
                pe.matmul(turn_bank[0:4 * TB, 0:P], shift[:, pair % OCT_PAIRS, :, :].rearrange("p x n -> p (x n)"), ident[:, :],
                          start=True, stop=True).then_inc(shift_turned, 1)

            def context(i, m, kt):
                if kt == 0:
                    if isinstance(i, int) and i == m == 0:
                        pe.wait_ge(job_evacuated, JOBS)
                    quad = QUADS * i + m
                    pe.wait_ge(probs_ready, TB * (HALF * quad + 3) + 1)
                    pe.wait_ge(v_ready, quad + 1)
                    pe.wait_ge(ctx_evacuated, quad)
                for h in range(HALF):
                    a, b = (h, kt) if m % 2 == 0 else (kt, h)
                    mm = pe.matmul(ctx_bank[32 * h:32 * h + 32, :], v_ring[:, m % 2, kt, h, :], probs[:, a, b, :],
                                   start=(kt == 0), stop=(kt == TB - 1))
                mm.then_inc(probs_used, 1)

            def scores(i, j, kt, first):
                e, slot = j // OCT, j % OCT
                if kt == 0 and j % 2 == 0:
                    pe.wait_ge(shift_loaded[slot // 2], 32 * i + 16 * e + 16)
                if first and j == 0 and kt < 2:
                    pe.wait_ge(job_evacuated, JOB_V + 6 + kt)
                else:
                    pe.wait_ge(probs_ready, TB * BODY * i + TB * j + kt - 1)
                pe.matmul(exp_tile[kt % 2], k_stack[e][0:ROWS_EXP, slot, kt * P:(kt + 1) * P],
                          q_stack[e][0:ROWS_EXP, slot, :], start=True, stop=True).then_inc(scores_ready, 1)

            def out_product(t, n):
                b, q = t // TB, (t % TB) * P
                a, m, c = [(a, m, c) for cs in (range(OPB - 2), (OPB - 2,), (OPB - 1,)) for a, m in ((0, 1), (1, 0), (0, 0)) for c in cs][n]
                mm = pe.matmul(bank[t], ctxs[a][:, OPB * b + c, q:q + P], oww[m][:, c, :], start=(n == 0), stop=(n == 3 * KC - 1))
                if n == 3 * KC - 1:
                    mm.then_inc(out_tile_ready, 1)

            def early_out_product(j, q):
                n = TB * (j - BODY + AHEAD) + q
                if n == 0:
                    pe.wait_ge(ow_ready, KC)
                    pe.wait_ge(ctx_split, OPB)
                if n % (3 * KC) == 0:
                    pe.wait_ge(maxes_ready, 2 * OCT * GROUPS - 1)
                out_product(n // (3 * KC), n % (3 * KC))

            def first_maxima(j):
                for q in range(TB):
                    max_scores(0, j, q, first=True)

            def step(i, j, first=False, last=False):
                to = j + AHEAD - (1 if first and j <= CATCH_UP else 0)
                ahead = None if last and to >= BODY else (i if to < BODY else i + 1, to % BODY)
                scores(i, j, 0, first)
                if ahead:
                    max_scores(*ahead, 0)
                else:
                    early_out_product(j, 0)
                scores(i, j, 1, first)
                if ahead:
                    for q in range(1, TB):
                        max_scores(*ahead, q)
                else:
                    for q in range(1, TB):
                        early_out_product(j, q)
                scores(i, j, 2, first)
                beside = turned_beside(i, j, first, last)
                if beside:
                    turn_shift(*beside)
                scores(i, j, 3, first)
                if first and j == CATCH_UP:
                    first_maxima(j + AHEAD)
                if j >= 3:
                    context(i, (j - 3) // HALF, (j - 3) % HALF)
                elif not first:
                    context(i - 1, QUADS - 1, j + 1)

            def v_product(t, part=range(3 * KC)):
                dst = begin(JOB_V + t) if part[0] == 0 else bank[BANK_OF[JOB_V + t]]
                mm = product(dst, lambda a, c: xt[a][:, c, t * P:(t + 1) * P], lambda m, c: w[m][:, c, 2 * H:3 * H], part)
                if part[-1] == 3 * KC - 1:
                    mm.then_inc(job_ready, 1)

            for t in range(5):
                v_product(t)
            v_product(5, range(0, 4))
            pe.wait_ge(pads_ready, 2)
            first_maxima(0)
            v_product(5, range(4, 12))
            first_maxima(1)
            v_product(6)
            first_maxima(2)
            turn_shift(0, 0)
            v_product(7, range(0, 6))
            first_maxima(3)
            v_product(7, range(6, 12))
            for j in range(BODY):
                if j == OCT - AHEAD + 1:
                    pe.wait_ge(pads_copied, 16)
                    pe.wait_ge(pads_ready, 2 + OCT // 2)
                step(0, j, first=True)
            with pe.Fori(1, TURNS - 1) as i:
                for j in range(BODY):
                    step(i, j)
            for j in range(BODY):
                step(TURNS - 1, j, last=True)
            for kt in range(1, TB):
                pe.wait_ge(probs_ready, TB * (OCT * GROUPS - 1) + kt + 1)
                context(TURNS - 1, QUADS - 1, kt)

            pe.wait_ge(maxes_ready, 2 * OCT * GROUPS)
            for n in range(TB * AHEAD, TB * 3 * KC):
                out_product(n // (3 * KC), n % (3 * KC))
            pe.wait_ge(ctx_split, GROUPS - 2)
            pe.wait_ge(shift_copied, PAIRS * TURNS)
            pe.wait_ge(ctx_evacuated, 2 * GROUPS)
            for t in range(TB, T):
                for n in range(3 * KC // 2):
                    out_product(t, n)
            for t in range(TB, T):
                for n in range(3 * KC // 2, 3 * KC):
                    if t == TB and n % 3 == 0:
                        pe.wait_ge(ctx_split, GROUPS - 3 + n // 3)
                    out_product(t, n)

        @block.scalar
        def _(act):
            act.dma_start(cent_raw[:, :], cent).then_inc(cent_loaded, 16)
            act.dma_start(qkb_raw[:, :], qkvb[0:2 * H].rearrange("(c p) -> c p", p=P)).then_inc(cent_loaded, 16)
            act.dma_start(assign_b[:, :], assign.partition_broadcast(CL)).then_inc(small_loaded, 16)
            act.dma_start(fb_b[:, :], fb.partition_broadcast(P)).then_inc(small_loaded, 16)
            act.dma_start(row_bias[:, :], qkvb[2 * H:3 * H].partition_broadcast(P)).then_inc(small_loaded, 16)

            def split_weights(c):
                act.wait_ge(w_loaded[c], 16)
                nc.scalar.copy(w_hi[:, c, :], w_stage[:, c % 2, :]).then_inc(w_hi_ready, 1)

            def gate_exponential(t):
                act.wait_ge(job_evacuated, JOB_DENSE[t] + 1)
                nc.scalar.activation(gate_exp[:, t, :], gate[:, t, :], ACT.Exp, scale=-1.0).then_inc(gate_exp_ready, 1)

            for n in SPLITS_A:
                act.wait_ge(job_ready, n + 1)
                src = bank[BANK_OF[n]]
                if n in JOB_WT:
                    dst = fwt_hi[:, JOB_WT.index(n), :]
                elif n == JOB_CENT:
                    dst, src = centt_hi[:, :, :].rearrange("p c k -> p (c k)"), src[:, 0:KC * CL]
                else:
                    t = JOB_XT.index(n)
                    dst, src = xt_hi[:, :, t * P:(t + 1) * P], src.rearrange("p (c q) -> p c q", c=KC)
                nc.scalar.copy(dst, src).then_inc(hi_ready, 1)
                if n == JOB_CENT:
                    split_weights(0)
                    split_weights(1)
                    gate_exponential(0)
            split_weights(2)
            gate_exponential(1)
            act.wait_ge(job_evacuated, JOB_LOGITS + 1)
            nc.scalar.activation(expo[:, :, :], logit[:, :, :], ACT.Exp, scale=SHARP).then_inc(exp_ready, 1)
            split_weights(3)
            for t in range(2, T):
                gate_exponential(t)
            for n, (g, which) in enumerate(qk_jobs):
                act.wait_ge(job_ready, JOB_QK + n + 1)
                col = which * KC + g % OPB
                nc.scalar.activation((q_hi, k_hi)[which][:, g, :], bank[BANK_OF[JOB_QK + n]], ACT.Identity,
                                     bias=qkb[:, col:col + 1]).then_inc(hi_ready, 1)

            def copy_shift(i, pair):
                act.wait_ge(shift_turned, PAIRS * i + pair + 1)
                if not (isinstance(i, int) and i == 0 and pair < 2):
                    octet, slot = (pair - 2) // OCT_PAIRS, (pair - 2) % OCT_PAIRS
                    act.wait_ge(shift_loaded[slot], 32 * i + 16 * octet + 16)
                nc.scalar.copy(shift_row[:, pair % 2, :], turn_bank[0:4 * TB, 0:P]).then_inc(shift_copied, 1)

            def step(i, j, first=False, last=False):
                beside = turned_beside(i, j, first, last)
                for kt in range(TB):
                    act.wait_ge(scores_ready, TB * (BODY * i + j) + kt + 1)
                    a, b = (j % HALF, kt) if j // HALF % 2 == 0 else (kt, j % HALF)
                    nc.scalar.activation(probs[:, a, b, :], exp_tile[kt % 2], ACT.Exp, scale=SCALE).then_inc(probs_ready, 1)
                    if kt == 2 and beside:
                        copy_shift(*beside)
                if last and j < KC:
                    if j == 0:
                        act.wait_ge(late_loaded, 16 * (OPB + 1 + T))
                        act.wait_ge(v_ready, QUADS * TURNS // B)
                    nc.scalar.copy(ow_hi[:, j, :], ow_raw[:, j, :]).then_inc(ow_hi_ready, 1)

            act.wait_ge(parts_stored[2], 64 * (GROUPS - 2))
            copy_shift(0, 0)
            for j in range(BODY):
                step(0, j, first=True)
            with act.Fori(1, TURNS - 1) as i:
                for j in range(BODY):
                    step(i, j)
            for j in range(BODY):
                step(TURNS - 1, j, last=True)
            for c in range(2):
                act.wait_ge(ctx_divided, GROUPS - 1 + c)
                nc.scalar.copy(ctx_hi[:, GROUPS - 2 + c, :], inv_b[:, c, :]).then_inc(ctx_hi_ready, 1)

        @block.vector
        def _(dve):
            steps = [0]

            def link(ins):
                steps[0] += 1
                ins.then_inc(dve_step, 1)
                dve.wait_ge(dve_step, steps[0])

            def statistics(t):
                dve.wait_ge(x_loaded[t], 16)
                nc.vector.bn_stats(stats[:, t, :], xn[:, t, :]).then_inc(stats_done, 1)
                dve.wait_ge(stats_done, t + 1)
                nc.vector.bn_aggr(mv[:, t, :], stats[:, t, :]).then_inc(aggr_done, 1)
                dve.wait_ge(aggr_done, t + 1)
                nc.vector.tensor_scalar_add(var_eps[:, t:t + 1], mv[:, t, 1:2], EPS).then_inc(var_ready, 1)

            def normalise(t):
                dve.wait_ge(rstd_ready, t + 1)
                nc.vector.tensor_scalar(xn[:, t, :], xn[:, t, :], mv[:, t, 0:1], rstd[:, t:t + 1],
                                        ALU.subtract, ALU.mult).then_inc(xn_ready, 1)

            def layer_norm(b):
                for t in range(TB * b, TB * (b + 1)):
                    statistics(t)
                    if t > TB * b:
                        normalise(t - 1)
                normalise(TB * (b + 1) - 1)

            def evacuated(ins):
                ins.then_inc(job_evacuated, 1)

            def split(n):
                dve.wait_ge(hi_ready, SPLITS_A.index(n) + 1)
                src = bank[BANK_OF[n]]
                if n in JOB_WT:
                    hi, lo = (h[:, JOB_WT.index(n), :] for h in (fwt_hi, fwt_lo))
                elif n == JOB_CENT:
                    link(nc.vector.tensor_copy(qkb[:, :], src[:, KC * CL:KC * CL + 2 * KC]))
                    src = src[:, 0:KC * CL]
                    hi, lo = (h[:, :, :].rearrange("p c k -> p (c k)") for h in (centt_hi, centt_lo))
                else:
                    t = JOB_XT.index(n)
                    hi, lo = (h[:, :, t * P:(t + 1) * P] for h in (xt_hi, xt_lo))
                    src = src.rearrange("p (c q) -> p c q", c=KC)
                evacuated(nc.vector.tensor_tensor(lo, src, hi.bitcast(F32), ALU.subtract))

            def evacuate_logits_t(b):
                dve.wait_ge(job_ready, JOB_LOGITS_T[b] + 1)
                evacuated(nc.vector.tensor_copy(logit_t[:, TB * b:TB * (b + 1), :].rearrange("p t q -> p (t q)"),
                                                bank[BANK_OF[JOB_LOGITS_T[b]]][0:CL, :]))

            def evacuate_dense(t):
                dve.wait_ge(job_ready, JOB_DENSE[t] + 1)
                evacuated(nc.vector.tensor_tensor(gate[:, t, :], bank[BANK_OF[JOB_DENSE[t]]], fb_b[:, :], ALU.add))

            def mask(t):
                dve.wait_ge(gate_exp_ready, t + 1)
                nc.vector.scalar_tensor_tensor(gate[:, t, :], gate[:, t, :], q_sel[:, t:t + 1], row_sel[:, :],
                                               ALU.mult, ALU.mult).then_inc(masked_ready, 1)

            def invert_gate(t):
                dve.wait_ge(gate_den_ready, t + 1)
                nc.vector.reciprocal(gate_exp[:, t, :], gate_exp[:, t, :]).then_inc(gate_inverted, 1)

            layer_norm(0)
            for n in SPLITS_A[:-TB]:
                split(n)
            layer_norm(1)
            dve.wait_ge(small_loaded, 48)
            evacuate_dense(0)
            evacuate_dense(1)
            evacuate_logits_t(0)
            evacuate_dense(2)
            for n in JOB_XT[TB:]:
                split(n)
            evacuate_dense(TB - 1)
            dve.wait_ge(iota_ready, 1)
            link(nc.vector.tensor_copy(iota_f[:, :], iota_i[:, :]))
            nc.vector.tensor_scalar(onehot[:, :], assign_b[:, :], iota_f[:, 0:1], None, ALU.is_equal).then_inc(onehot_ready, 1)
            evacuate_logits_t(1)
            evacuate_dense(4)
            dve.wait_ge(job_ready, JOB_LOGITS + 1)
            lg = bank[BANK_OF[JOB_LOGITS]].rearrange("p (t k) -> p t k", t=T)
            link(nc.vector.tensor_reduce(lmax[:, :], lg, AX.X, ALU.max))
            evacuated(nc.vector.tensor_tensor(logit[:, :, :], lg, lmax[:, :].unsqueeze(2).to_broadcast([P, T, CL]), ALU.subtract))
            dve.wait_ge(exp_ready, 1)
            link(nc.vector.tensor_reduce(thr[:, :], expo[:, :, :], AX.X, ALU.add))
            link(nc.vector.tensor_scalar(thr[:, :], thr[:, :], HIT, None, ALU.mult))
            nc.vector.tensor_tensor(hits[:, :, :], expo[:, :, :], thr[:, :].unsqueeze(2).to_broadcast([P, T, CL]),
                                    ALU.is_gt).then_inc(hits_ready, 1)
            dve.wait_ge(hits_ready, 1)
            link(nc.vector.tensor_reduce(q_sel[:, :], hits[:, :, :], AX.X, ALU.max))
            evacuate_dense(5)
            evacuate_dense(6)
            dve.wait_ge(job_ready, JOB_COUNT + 1)
            evacuated(nc.vector.tensor_scalar(cl_sel[:, :], bank[BANK_OF[JOB_COUNT]][0:CL, 0:P], 0.5, None, ALU.is_gt))
            invert_gate(0)
            evacuate_dense(7)
            dve.wait_ge(job_ready, JOB_ROWSEL + 1)
            evacuated(nc.vector.tensor_copy(row_sel[:, :], bank[BANK_OF[JOB_ROWSEL]]))
            dve.wait_ge(job_evacuated, JOB_ROWSEL + 1)
            for n, (g, which) in enumerate(qk_jobs):
                dve.wait_ge(hi_ready, len(SPLITS_A) + n + 1)
                col = which * KC + g % OPB
                evacuated(nc.vector.scalar_tensor_tensor(
                    (q_lo, k_lo)[which][:, g, :], bank[BANK_OF[JOB_QK + n]], qkb[:, col:col + 1],
                    (q_hi, k_hi)[which][:, g, :].bitcast(F32), ALU.add, ALU.subtract))
                t = n // 3 * 2 + n % 3
                if n % 3 < 2 and t < T:
                    if t > 0:
                        invert_gate(t)
                    mask(t)

            def invert(i):
                for r in range(2):
                    dve.wait_ge(den_loaded[r], 16 * i + 16)
                nc.vector.reciprocal(den[:, :, :], den[:, :, :]).then_inc(den_inverted, 1)

            def evacuate(i, m):
                dve.wait_ge(probs_used, TB * (QUADS * i + m + 1))
                if m % 2 == 0 and not (isinstance(i, int) and i == m == 0):
                    octet = (m // 2 + 1) % 2
                    dve.wait_ge(den_loaded[octet], 16 * (i + m // 2))
                    dve.wait_ge(ctx_packed[octet], PACK * (i + m // 2))
                nc.vector.tensor_copy(ctx_raw[:, m % 2, :], ctx_bank).then_inc(ctx_evacuated, 1)

            def context_hi(i, c):
                dve.wait_ge(ctx_divided, 2 * i + c + 1)
                nc.vector.tensor_copy(ctx_hi[:, bass.ds(2 * i + c, 1), :].rearrange("p a s -> p (a s)"), inv_b[:, c, :]).then_inc(ctx_hi_ready, 1)

            def maxima(i, heads, first=False):
                for j in heads:
                    if j % 2 == 0 and not (first and j < OCT):
                        dve.wait_ge(shift_split, PAIRS * i + j // 2 + 1 - OCT_PAIRS)
                    for u in range(2):
                        dve.wait_ge(max_scores_ready, 2 * (BODY * i + j) + u + 1)
                        nc.vector.tensor_reduce(neg_max[:, j % OCT, 2 * u:2 * u + 2], max_tile[u][:, :, :], AX.X, ALU.max,
                                                negate=True).then_inc(maxes_ready, 1)
                    if j % HALF == 3 and not (first and j < OCT):
                        m = j // HALF - 2
                        evacuate(i if m >= 0 else i - 1, m % QUADS)
                    if not first:
                        if j == 9:
                            invert(i - 1)
                        if j in (13, 14):
                            context_hi(i - 1, j - 13)

            def evacuate_v(t):
                b, kt = t // TB, t % TB
                dve.wait_ge(job_ready, JOB_V + t + 1)
                evacuated(nc.vector.tensor_tensor(
                    v_all[:, b * OPB:(b + 1) * OPB, kt, :], bank[BANK_OF[JOB_V + t]].rearrange("p (o c) -> p o c", o=OPB),
                    row_bias[:, :].rearrange("p (o c) -> p o c", o=OPB), ALU.add))

            dve.wait_ge(gate_ready, T)
            for t in range(5):
                evacuate_v(t)
            for j in range(4):
                maxima(0, (j,), first=True)
                if j != 2:
                    evacuate_v(5 + (j + 1) // 2)
            maxima(0, range(4, BODY), first=True)
            with dve.Fori(1, TURNS) as i:
                maxima(i, range(BODY))

            def finish(t):
                dve.wait_ge(out_tile_ready, t + 1)
                nc.vector.tensor_tensor(gate[:, t, :], bank[t], gate[:, t, :], ALU.mult).then_inc(gated_ready, 1)
                dve.wait_ge(gated_ready, t + 1)
                dve.wait_ge(rest_ready, t + 1)
                nc.vector.tensor_tensor(x_res[:, t, :], x_res[:, t, :], gate[:, t, :], ALU.add).then_inc(out_ready, 1)

            evacuate(TURNS - 1, QUADS - 2)
            finish(0)
            evacuate(TURNS - 1, QUADS - 1)
            dve.wait_ge(ctx_split, 2 * (TURNS - 1))
            invert(TURNS - 1)
            for t in range(1, TB):
                finish(t)
            dve.wait_ge(inv_loaded, 32 * TURNS)
            for r in range(2):
                dve.wait_ge(ctx_packed[r], PACK * TURNS)
            for c in range(2):
                nc.vector.tensor_tensor(inv_b[:, c, :], ctx_c[:, c, :], inv_b[:, c, :], ALU.mult).then_inc(ctx_divided, 1)
            for c in range(2):
                dve.wait_ge(ctx_hi_ready, 2 * TURNS - 1 + c)
                nc.vector.tensor_tensor(ctx_lo[:, GROUPS - 2 + c, :], inv_b[:, c, :], ctx_hi[:, GROUPS - 2 + c, :].bitcast(F32),
                                        ALU.subtract).then_inc(ctx_split, 1)
            for t in range(TB, T):
                finish(t)

        @block.gpsimd
        def _(pool):
            steps = [0]

            def link(ins):
                steps[0] += 1
                ins.then_inc(pool_step, 1)
                pool.wait_ge(pool_step, steps[0])

            nc.gpsimd.memset(neg_half[:, :], -0.5)
            nc.gpsimd.memset(zeros[:, :], 0.0)
            link(nc.gpsimd.memset(ident[:, :], 0.0))
            nc.gpsimd.affine_select(out=ident[:, :], in_=ident[:, :], compare_op=ALU.not_equal, fill=1.0, base=0,
                                    pattern=[[-1, P]], channel_multiplier=1).then_inc(consts_ready, 1)
            nc.gpsimd.iota(iota_i[:, :], [[0, 1]], base=0, channel_multiplier=1).then_inc(iota_ready, 1)
            link(nc.gpsimd.memset(ones_bf[:, :], 1.0))
            for t in range(T):
                pool.wait_ge(var_ready, t + 1)
                nc.gpsimd.tensor_tensor(rstd[:, t:t + 1], var_eps[:, t:t + 1], neg_half[:, t:t + 1], ALU.pow).then_inc(rstd_ready, 1)

            def weights_lo(c):
                pool.wait_ge(w_hi_ready, c + 1)
                nc.gpsimd.tensor_tensor(w_lo[:, c, :], w_stage[:, c % 2, :], w_hi[:, c, :].bitcast(F32),
                                        ALU.subtract).then_inc(w_lo_ready, 1)

            def gate_denominator(t):
                pool.wait_ge(gate_exp_ready, t + 1)
                nc.gpsimd.tensor_scalar(gate_exp[:, t, :], gate_exp[:, t, :], 1.0, None, ALU.add).then_inc(gate_den_ready, 1)

            weights_lo(0)
            weights_lo(1)
            gate_denominator(0)
            weights_lo(2)
            weights_lo(3)
            for t in range(1, T):
                gate_denominator(t)
            for t in range(T):
                pool.wait_ge(gate_inverted, t + 1)
                pool.wait_ge(masked_ready, t + 1)
                nc.gpsimd.tensor_tensor(gate[:, t, :], gate[:, t, :], gate_exp[:, t, :], ALU.mult).then_inc(gate_ready, 1)
            pool.wait_ge(gate_ready, T)

            nc.gpsimd.memset(q_stack[0][4 * HD:ROWS_MAX, :, :].bitcast(F32), 0.0).then_inc(pads_ready, 1)
            pool.wait_ge(pads_ready, 1)
            pool.wait_ge(w_lo_ready, KC)
            pool.wait_ge(job_ready, JOB_V)
            nc.gpsimd.memset(k_stack[0][4 * HD:ROWS_EXP, :, :].bitcast(F32), 1.0).then_inc(pads_ready, 1)
            pool.wait_ge(pads_ready, 2)

            def split_shift(i, pair, first=False):
                done, slot = PAIRS * i + pair, pair % OCT_PAIRS
                pool.wait_ge(maxes_ready, 4 * done + 4)
                if not (first and pair < OCT_PAIRS):
                    pool.wait_ge(shift_turned, done + 1 - OCT_PAIRS)
                maxima = neg_max[:, 2 * slot:2 * slot + 2, :].rearrange("p h t -> p (h t)")
                nc.gpsimd.tensor_tensor(shift[:, slot, 0, :].bitcast(F32R), maxima, zeros[:, :], ALU.add).then_inc(shift_hi_ready, 1)
                pool.wait_ge(shift_hi_ready, done + 1)
                nc.gpsimd.tensor_tensor(shift[:, slot, 1, :], maxima, shift[:, slot, 0, :], ALU.subtract).then_inc(shift_split, 1)

            def group(buffer, g):
                return buffer[:, bass.ds(g, 1), :].rearrange("p a s -> p (a s)")

            def fill_v(i, m):
                quad, e = QUADS * i + m, m % 2
                if not (isinstance(i, int) and quad < 2):
                    pool.wait_ge(probs_used, TB * (quad - 1))
                cols = slice(HALF * HD * e, HALF * HD * (e + 1))
                nc.gpsimd.tensor_copy(
                    v_ring[:, e, :, :, 0:HD],
                    v_all[:, bass.ds(2 * i + m // 2, 1), :, cols].rearrange("p a t (h d) -> p (a t) h d", d=HD)).then_inc(v_ready, 1)

            def divide(i, c):
                if c == 0:
                    pool.wait_ge(inv_loaded, 32 * i + 32)
                    for r in range(2):
                        pool.wait_ge(ctx_packed[r], PACK * i + PACK)
                nc.gpsimd.tensor_tensor(inv_b[:, c, :], ctx_c[:, c, :], inv_b[:, c, :], ALU.mult).then_inc(ctx_divided, 1)

            def context_lo(i, c):
                pool.wait_ge(ctx_hi_ready, 2 * i + c + 1)
                nc.gpsimd.tensor_tensor(group(ctx_lo, 2 * i + c), inv_b[:, c, :], group(ctx_hi, 2 * i + c).bitcast(F32),
                                        ALU.subtract).then_inc(ctx_split, 1)

            def output_weights_lo(c):
                pool.wait_ge(ow_hi_ready, c + 1)
                nc.gpsimd.tensor_tensor(ow_lo[:, c, :], ow_raw[:, c, :], ow_hi[:, c, :].bitcast(F32), ALU.subtract).then_inc(ow_ready, 1)

            def residual(t, half):
                if half == 0:
                    if t == 0:
                        pool.wait_ge(late_loaded, 16 * (OPB + 1 + T))
                    else:
                        pool.wait_ge(rest_ready, t)
                    nc.gpsimd.tensor_tensor(ob_gate[:, :], ob_b[:, :], gate[:, t, :], ALU.mult).then_inc(bias_gated, 1)
                else:
                    pool.wait_ge(bias_gated, t + 1)
                    nc.gpsimd.tensor_tensor(x_res[:, t, :], x_res[:, t, :], ob_gate[:, :], ALU.add).then_inc(rest_ready, 1)

            def steps_of(i, first=False, last=False):
                for j in range(BODY):
                    if j % 2:
                        split_shift(i, j // 2, first)
                    if first and j == 3:
                        pool.wait_ge(shift_split, (j + 1) // 2)
                        pool.wait_ge(job_ready, JOBS)
                        nc.gpsimd.memset(v_ring[:, :, :, :, HD:2 * HD], 1.0).then_inc(ones_ready, 1)
                        pool.wait_ge(ones_ready, 1)
                    if first and 3 <= j < 3 + OCT // 2:
                        pool.wait_ge(shift_split, (j + 1) // 2)
                        n = j - 3
                        if j == 6:
                            pool.wait_ge(v_ready, 1)
                        nc.gpsimd.memset(q_stack[1][4 * HD:ROWS_MAX, 2 * n:2 * n + 2, :].bitcast(F32), 0.0).then_inc(pads_ready, 1)
                        pool.wait_ge(pads_ready, 3 + n)
                    if j % HALF == 1 and not (first and j == 1):
                        m = j // HALF - 1
                        fill_v(i if m >= 0 else i - 1, m % QUADS)
                    if not first:
                        if j in (12, 13):
                            divide(i - 1, j - 12)
                        if j >= 14:
                            context_lo(i - 1, j - 14)
                    if last:
                        residual(j // 2, j % 2)
                        if j in (6, 7, 8, 10):
                            output_weights_lo((6, 7, 8, 10).index(j))

            steps_of(0, first=True)
            with pool.Fori(1, TURNS - 1) as i:
                steps_of(i)
            steps_of(TURNS - 1, last=True)
            fill_v(TURNS - 1, QUADS - 1)


_INS = ["L0_attn_x", "L0_attn_attn_qkvw", "L0_attn_attn_qkvb", "L0_attn_attn_ow", "L0_attn_attn_ob",
        "L0_ffn_weight", "L0_ffn_bias", "L0_ffn_centroids", "L0_ffn_assignments"]


def kernel(**inputs):
    import numpy as _np
    import concourse.bacc as _bacc
    from concourse import mybir as _mybir
    from concourse.bass_utils import run_bass_kernel_spmd as _run

    nc = _bacc.Bacc("TRN2", target_bir_lowering=False, num_devices=1)
    arrays, args = {}, []
    for name in _INS:
        a = _np.ascontiguousarray(inputs[name])
        arrays[f"in_{name}"] = a
        args.append(nc.dram_tensor(f"in_{name}", a.shape, _mybir.dt.from_np(a.dtype), kind="ExternalInput").ap())
    shape = arrays["in_L0_attn_x"].shape
    out = nc.dram_tensor("out_x", shape, _mybir.dt.float32, kind="ExternalOutput").ap()
    build(nc, *args, out)
    r = _run(nc, [arrays], core_ids=[0])
    return r.results[0]["out_x"]
```
